# Optimizing a Trainium2 kernel written in Bass

```python
import numpy as np
import jax
import jax.numpy as jnp

def _softmax(x, axis=-1):
    return jax.nn.softmax(x, axis=axis)

def _gelu(x):
    return jax.nn.gelu(x, approximate=True)

def _silu(x):
    return jax.nn.silu(x)

def _sigmoid(x):
    return jax.nn.sigmoid(x)

def _layernorm(x, axis=-1, eps=1e-05):
    m = jnp.mean(x, axis=axis, keepdims=True)
    v = jnp.var(x, axis=axis, keepdims=True)
    return (x - m) / jnp.sqrt(v + eps)

def _scatter_add(tgt, idx, src, axis=0):
    return tgt.at[idx].add(src)

def _segment_sum(src, seg, n):
    return jax.ops.segment_sum(src, seg, n)
kernel_name = 'mk_adj_preln_d2_adj_r2_9c7a8c'

def setup_inputs(seed: int=0):
    np.random.seed(seed)
    _w = jnp.asarray

    def _rec_inputs():
        import jax
        import jax.numpy as jnp
        _gk = jax.random.key(seed)
        x = -0.0005963 + 1.001 * jax.random.normal(jax.random.fold_in(_gk, 1), (128, 64, 384), jnp.float32)
        _w = (1.0 + jnp.arange(64, dtype=jnp.float32)) ** (-0.5)
        _w = _w / _w.mean()
        _pij = jnp.clip(0.125 * _w[:, None] * _w[None, :], 0.0, 1.0)
        _a = jax.random.uniform(jax.random.fold_in(_gk, 2), (128, 64, 64)) < _pij
        adj = _a
        return (x, adj)
    x, adj = _rec_inputs()

    def _L0_gnn_setup():
        import jax, jax.numpy as jnp
        import numpy as np
        ATT_HEAD = 12
        IN_DIM = 384
        OUT_DIM = IN_DIM // ATT_HEAD
        LEAKY_ALPHA = 0.2
        B, N = (8, 256)
        key = jax.random.key(seed)
        ks = jax.random.split(key, 8)
        feat_in = jax.random.normal(ks[0], (B, N, IN_DIM), dtype=jnp.float32)
        adj = jax.random.randint(ks[1], (B, N, N), 0, 2) > 0
        lim_W = float(np.sqrt(6.0 / (IN_DIM + OUT_DIM)))
        W = jax.random.uniform(ks[2], (ATT_HEAD, IN_DIM, OUT_DIM), minval=-lim_W, maxval=lim_W, dtype=jnp.float32)
        b = jnp.zeros((OUT_DIM,), dtype=jnp.float32)
        lim_w = float(np.sqrt(6.0 / (OUT_DIM + 1)))
        w_src = jax.random.uniform(ks[3], (ATT_HEAD, OUT_DIM, 1), minval=-lim_w, maxval=lim_w, dtype=jnp.float32)
        w_dst = jax.random.uniform(ks[4], (ATT_HEAD, OUT_DIM, 1), minval=-lim_w, maxval=lim_w, dtype=jnp.float32)
        std_H = float(np.sqrt(2.0 / (IN_DIM + IN_DIM)))
        H_w = jax.random.normal(ks[5], (IN_DIM, IN_DIM), dtype=jnp.float32) * std_H
        H_b = jax.random.normal(ks[6], (IN_DIM,), dtype=jnp.float32) * 0.01
        return {'feat_in': feat_in, 'adj': adj, 'W': W, 'b': b, 'w_src': w_src, 'w_dst': w_dst, 'H_w': H_w, 'H_b': H_b}
    _L0_gnn_all = _L0_gnn_setup()
    _L0_gnn_in = {k: v for k, v in _L0_gnn_all.items() if k in ('W', 'b', 'w_src', 'w_dst', 'H_w', 'H_b')}
    del _L0_gnn_all

    def _L1_gnn_setup():
        import jax, jax.numpy as jnp
        import numpy as np
        B, S, H = (4, 1024, 384)
        NUM_HEADS = 6
        HEAD_SIZE = H // NUM_HEADS
        NEG = -9000000000000000.0

        def _heads(x):
            b, s, _ = x.shape
            return x.reshape(b, s, NUM_HEADS, HEAD_SIZE).transpose(0, 2, 1, 3)
        key = jax.random.key(seed)
        ks = jax.random.split(key, 10)
        seq_inputs = jax.random.normal(ks[0], (B, S, H), dtype=jnp.float32)
        gm = jax.random.randint(ks[1], (B, S, S), 0, 2) > 0
        graph_mask = gm | jnp.eye(S, dtype=bool)[None]
        sc = 1.0 / np.sqrt(H)
        Wq = jax.random.normal(ks[2], (H, H), dtype=jnp.float32) * sc
        bq = jnp.zeros((H,), dtype=jnp.float32)
        Wk = jax.random.normal(ks[3], (H, H), dtype=jnp.float32) * sc
        bk = jnp.zeros((H,), dtype=jnp.float32)
        Wv = jax.random.normal(ks[4], (H, H), dtype=jnp.float32) * sc
        bv = jnp.zeros((H,), dtype=jnp.float32)
        Wf = jax.random.normal(ks[5], (H, H), dtype=jnp.float32) * sc
        bf = jnp.zeros((H,), dtype=jnp.float32)
        return {'seq_inputs': seq_inputs, 'Wq': Wq, 'bq': bq, 'Wk': Wk, 'bk': bk, 'Wv': Wv, 'bv': bv, 'Wf': Wf, 'bf': bf, 'graph_mask': graph_mask}
    _L1_gnn_all = _L1_gnn_setup()
    _L1_gnn_in = {k: v for k, v in _L1_gnn_all.items() if k in ('Wq', 'bq', 'Wk', 'bk', 'Wv', 'bv', 'Wf', 'bf')}
    del _L1_gnn_all
    return {'x': x, 'adj': adj, 'L0_gnn_W': _L0_gnn_in['W'], 'L0_gnn_b': _L0_gnn_in['b'], 'L0_gnn_w_src': _L0_gnn_in['w_src'], 'L0_gnn_w_dst': _L0_gnn_in['w_dst'], 'L0_gnn_H_w': _L0_gnn_in['H_w'], 'L0_gnn_H_b': _L0_gnn_in['H_b'], 'L1_gnn_Wq': _L1_gnn_in['Wq'], 'L1_gnn_bq': _L1_gnn_in['bq'], 'L1_gnn_Wk': _L1_gnn_in['Wk'], 'L1_gnn_bk': _L1_gnn_in['bk'], 'L1_gnn_Wv': _L1_gnn_in['Wv'], 'L1_gnn_bv': _L1_gnn_in['bv'], 'L1_gnn_Wf': _L1_gnn_in['Wf'], 'L1_gnn_bf': _L1_gnn_in['bf']}

def reference(x, adj, L0_gnn_W, L0_gnn_b, L0_gnn_w_src, L0_gnn_w_dst, L0_gnn_H_w, L0_gnn_H_b, L1_gnn_Wq, L1_gnn_bq, L1_gnn_Wk, L1_gnn_bk, L1_gnn_Wv, L1_gnn_bv, L1_gnn_Wf, L1_gnn_bf):
    import jax
    import jax.numpy as jnp

    def _L0_gnn_ref(feat_in, adj, W, b, w_src, w_dst, H_w, H_b):
        import jax, jax.numpy as jnp
        import numpy as np
        ATT_HEAD = 12
        IN_DIM = 384
        OUT_DIM = IN_DIM // ATT_HEAD
        LEAKY_ALPHA = 0.2
        B, N = (8, 256)
        h = jnp.einsum('bnd,ade->bane', feat_in, W)
        th = jnp.tanh(h)
        attn_src = jnp.einsum('bane,aeo->bano', th, w_src)
        attn_dst = jnp.einsum('bane,aeo->bano', th, w_dst)
        attn = attn_src + jnp.swapaxes(attn_dst, 2, 3)
        attn = jnp.where(attn >= 0, attn, LEAKY_ALPHA * attn)
        mask = ~adj[:, None, :, :]
        attn = jnp.where(mask, jnp.float32(-999.0), attn)
        attn = jax.nn.softmax(attn, axis=-1)
        feat_out = jnp.einsum('banm,bame->bane', attn, h) + b
        feat_out = jnp.swapaxes(feat_out, 1, 2).reshape(feat_in.shape[0], feat_in.shape[1], -1)
        feat_out = jax.nn.elu(feat_out)
        gate = jax.nn.sigmoid(feat_in @ H_w.T + H_b)
        return gate * feat_out + (1.0 - gate) * feat_in

    def _L1_gnn_ref(seq_inputs, Wq, bq, Wk, bk, Wv, bv, Wf, bf, graph_mask):
        import jax, jax.numpy as jnp
        import numpy as np
        B, S, H = (4, 1024, 384)
        NUM_HEADS = 6
        HEAD_SIZE = H // NUM_HEADS
        NEG = -9000000000000000.0

        def _heads(x):
            b, s, _ = x.shape
            return x.reshape(b, s, NUM_HEADS, HEAD_SIZE).transpose(0, 2, 1, 3)
        q = _heads(seq_inputs @ Wq + bq)
        k = _heads(seq_inputs @ Wk + bk)
        v = _heads(seq_inputs @ Wv + bv)
        scores = jnp.einsum('bhqd,bhkd->bhqk', q, k) / np.sqrt(HEAD_SIZE)
        bias = jnp.where(graph_mask, 0.0, NEG)[:, None]
        probs = jax.nn.softmax(scores + bias, axis=-1)
        ctx = jnp.einsum('bhqk,bhkd->bhqd', probs, v)
        ctx = ctx.transpose(0, 2, 1, 3).reshape(seq_inputs.shape[0], seq_inputs.shape[1], H)
        return ctx @ Wf + bf
    h = jnp.maximum(_layernorm(x, axis=-1), 0.0)
    x = x + _L0_gnn_ref(h, adj, L0_gnn_W, L0_gnn_b, L0_gnn_w_src, L0_gnn_w_dst, L0_gnn_H_w, L0_gnn_H_b)
    h = jnp.maximum(_layernorm(x, axis=-1), 0.0)
    x = x + _L1_gnn_ref(h, L1_gnn_Wq, L1_gnn_bq, L1_gnn_Wk, L1_gnn_bk, L1_gnn_Wv, L1_gnn_bv, L1_gnn_Wf, L1_gnn_bf, adj)
    return x

_drawn_inputs = setup_inputs


def setup_inputs(seed=0):
    import zlib

    import numpy as np

    out = dict(_drawn_inputs(seed))
    spreads = {'L0_gnn_b': (0.0, 0.1),
     'L1_gnn_bq': (0.0, 0.797),
     'L1_gnn_bk': (0.0, 2.0),
     'L1_gnn_bv': (0.0, 0.1),
     'L1_gnn_bf': (0.0, 0.1)}
    factors = {'L0_gnn_w_src': 3.582, 'L0_gnn_H_b': 34.27}
    for name, (base, spread) in spreads.items():
        noise = np.random.default_rng([zlib.crc32(name.encode()), seed]).standard_normal(out[name].shape)
        drawn = base * np.exp(spread * noise) if base else spread * noise
        out[name] = jnp.asarray(drawn.astype(out[name].dtype))
    for name, factor in factors.items():
        out[name] = (out[name] * factor).astype(out[name].dtype)
    return out
```

```python
from contextlib import ExitStack

import numpy as np

import concourse.bass as bass
from concourse import mybir

ACT = mybir.ActivationFunctionType
ALU = mybir.AluOpType
AX_X = mybir.AxisListType.X
F32 = mybir.dt.float32
F32R = mybir.dt.float32r
BF16 = mybir.dt.bfloat16
U8 = mybir.dt.uint8

P = 128
N = 64
D = 384
C = D // P
TILES = 4
TOK = TILES * P
HEADS0, E0 = 12, 32
HEADS1, E1 = 6, 64
PAIRS0, PAIRS1 = HEADS0 // 2, HEADS1 // 2
BANKS = 8
SLOPE = 0.2
MASKED0 = -999.0
MASKED1 = 9e15
EPS = 1e-5

def two_layer_gnn(nc, x, adj, W0, b0, w_src, w_dst, H_w, H_b, Wq, bq, Wk, bk, Wv, bv, Wf, bf, out, d_scratch):
    groups = x.shape[0] * x.shape[1] // TOK
    x_v = x.rearrange("a n d -> (a n) d").rearrange("(i t p) d -> i p t d", t=TILES, p=P)
    out_v = out.rearrange("a n d -> (a n) d").rearrange("(i t p) d -> i p t d", t=TILES, p=P)
    adj_v = adj.rearrange("a n m -> (a n) m").rearrange("(i t p) m -> i p t m", t=TILES, p=P)

    with ExitStack() as ctx:
        def sb(name, shape, dt=F32):
            return ctx.enter_context(nc.sbuf_tensor(name, shape, dt))

        def sem(name):
            return ctx.enter_context(nc.semaphore(name))

        wh = {k: sb(f"{k}_hi", [P, C, D], F32R) for k in ("W0", "Hw", "Wq", "Wk", "Wv", "Wf")}
        wl = {k: sb(f"{k}_lo", [P, C, D], F32R) for k in ("W0", "Hw", "Wq", "Wk", "Wv", "Wf")}
        wsd = sb("wsd", [P, C, 2 * HEADS0])
        hb_rows = sb("hb_rows", [33, D], F32R)
        ones_rows = sb("ones_rows", [33, P], F32R)
        b0_plus1 = sb("b0_plus1", [P, E0])
        bq_col = sb("bq_col", [P, C])
        bk_col = sb("bk_col", [P, C])
        bv_row = sb("bv_row", [P, D])
        bf_row = sb("bf_row", [P, D])
        ident = sb("ident", [P, P])
        ident_b = sb("ident_b", [P, P], BF16)
        masked0 = sb("masked0", [P, 1])
        minus1 = sb("minus1", [P, 1])
        half = sb("half", [P, 1])
        minus_half = sb("minus_half", [P, TILES])

        x_in = sb("x_in", [P, 2, TILES, D])
        xn0 = sb("xn0", [P, 2, TILES, D])
        adj_in = sb("adj_in", [P, 2, TILES, N], U8)
        hT0h = sb("hT0h", [P, C, TOK], F32R)
        hT0l = sb("hT0l", [P, C, TOK], F32R)
        hT1h = sb("hT1h", [P, C, TOK], F32R)
        hT1l = sb("hT1l", [P, C, TOK], F32R)
        gate = sb("gate", [P, TILES, D])
        V0 = sb("V0", [P, TILES, HEADS0, E0 + 1])
        V0s = sb("V0s", [P, TILES, HEADS0, E0 + 1])
        thT = sb("thT", [P, C, TOK])
        sdT = sb("sdT", [2 * HEADS0, TOK])
        s_tok = sb("s_tok", [P, TILES, 2 * HEADS0])
        z = sb("z", [P, TILES, HEADS0 * N])
        big = sb("big", [P, 6, TOK])
        x1 = sb("x1", [P, TILES, D])
        ee = sb("ee", [P, TILES, D])
        x2 = sb("x2", [P, TILES, D])
        V1 = sb("V1", [P, TILES, HEADS1, E1 + 1])
        V1s = sb("V1s", [P, TILES, HEADS1, E1 + 1])
        p1 = sb("p1", [P, TILES, D])
        not_adj = sb("not_adj", [P, TILES, N], U8)
        mask1 = sb("mask1", [P, TILES, N], BF16)
        mx0 = sb("mx0", [P, TILES, HEADS0])
        rs0 = sb("rs0", [P, TILES, HEADS0])
        mx1 = sb("mx1", [P, TILES, HEADS1])
        rs1 = sb("rs1", [P, TILES, HEADS1])
        stats = sb("stats", [P, 2, TILES, 6])
        mv = sb("mv", [P, 2, TILES, 2])
        ve = sb("ve", [P, 2, TILES])
        rstd = sb("rstd", [P, 2, TILES])
        ps = ctx.enter_context(nc.psum_tensor("ps", [P, BANKS, 512], F32))
        stage_w = big[:, 0:3, 0:D]
        stage_h = x1

        hw_loaded = sem("hw_loaded")
        consts_loaded = sem("consts_loaded")
        consts_made = sem("consts_made")
        small_ready = sem("small_ready")
        w_high = sem("w_high")
        w_low = sem("w_low")
        hw_turned = sem("hw_turned")
        zeros_made = sem("zeros_made")
        rows_made = sem("rows_made")
        w_loaded = [sem("w_loaded_0"), sem("w_loaded_1")]
        x_loaded = sem("x_loaded")
        values0_swapped = sem("values0_swapped")
        values1_swapped = sem("values1_swapped")
        dst_stored = sem("dst_stored")
        dst_spread = sem("dst_spread")
        out_stored = sem("out_stored")
        adj_loaded = [sem("adj_loaded_0"), sem("adj_loaded_1")]
        xn0_turned = sem("xn0_turned")
        values0_full = sem("values0_full")
        gate_full = sem("gate_full")
        xn1_turned = sem("xn1_turned")
        q_full = sem("q_full")
        k_full = sem("k_full")
        values1_full = sem("values1_full")
        th_turned = sem("th_turned")
        srcdst_full = sem("srcdst_full")
        srcdst_turned = sem("srcdst_turned")
        scores1_full = sem("scores1_full")
        probs1_turned = sem("probs1_turned")
        attn1_full = sem("attn1_full")
        attn1_turned = sem("attn1_turned")
        final_full = sem("final_full")
        probs0_turned = sem("probs0_turned")
        attn0_full = sem("attn0_full")
        h0_high = sem("h0_high")
        th_made = sem("th_made")
        gate_tanh = sem("gate_tanh")
        gate_made = sem("gate_made")
        h1_high = sem("h1_high")
        q_copied = sem("q_copied")
        k_copied = sem("k_copied")
        thT_copied = sem("thT_copied")
        srcdst_copied = sem("srcdst_copied")
        probs1_made = sem("probs1_made")
        probs1T_copied = sem("probs1T_copied")
        attn1_high = sem("attn1_high")
        probs0_made = sem("probs0_made")
        probs0T_copied = sem("probs0T_copied")
        elu_exp = sem("elu_exp")
        stats0 = sem("stats0")
        moments0 = sem("moments0")
        xn0_made = sem("xn0_made")
        h0_low = sem("h0_low")
        values0_made = sem("values0_made")
        h1_low = sem("h1_low")
        values1_made = sem("values1_made")
        src_copied = sem("src_copied")
        max1_made = sem("max1_made")
        scores1_shifted = sem("scores1_shifted")
        masks_made = sem("masks_made")
        leaky_made = sem("leaky_made")
        masked = sem("masked")
        max0_made = sem("max0_made")
        scores0_shifted = sem("scores0_shifted")
        inv1_made = sem("inv1_made")
        attn1_made = sem("attn1_made")
        attn1_low = sem("attn1_low")
        out_made = sem("out_made")
        inv0_made = sem("inv0_made")
        attn0_made = sem("attn0_made")
        elu_made = sem("elu_made")
        h_less_elu = sem("h_less_elu")
        x_plus_h = sem("x_plus_h")
        gated = sem("gated")
        stats1 = sem("stats1")
        moments1 = sem("moments1")
        xn1_made = sem("xn1_made")
        scores0_summed = sem("scores0_summed")
        var0_eps = sem("var0_eps")
        inv_std0 = sem("inv_std0")
        x2_made = sem("x2_made")
        var1_eps = sem("var1_eps")
        inv_std1 = sem("inv_std1")
        x2_biased = sem("x2_biased")
        sp_passed = sem("sp_passed")
        pool_passed = sem("pool_passed")
        pe_passed = sem("pe_passed")
        dve_passed = sem("dve_passed")

        def real(g):
            return not isinstance(g, int) or 0 <= g < groups

        def jobs(name, layer, signal, n):
            return [(name, layer, signal, n, k) for k in range(n)]

        pairs_of_jobs = zip(jobs("th_made", 0, th_made, 4), jobs("gate_tanh", 0, gate_tanh, 4))
        RING = (
            jobs("h0_low", 0, h0_low, 3)
            + [x for pair in pairs_of_jobs for x in pair]
            + jobs("h1_low", 1, h1_low, 3)
            + jobs("q_copied", 1, q_copied, 3)
            + jobs("k_copied", 1, k_copied, 3)
            + jobs("values1_made", 1, values1_made, 4)
            + jobs("thT_copied", 0, thT_copied, 3)
            + jobs("src_copied", 0, src_copied, 1)
            + jobs("scores1_shifted", 1, scores1_shifted, 4)
            + jobs("probs1T_copied", 1, probs1T_copied, 3)
            + jobs("attn1_made", 1, attn1_made, 4)
            + jobs("attn1_low", 1, attn1_low, 3)
            + jobs("out_made", 1, out_made, 4)
            + jobs("probs0T_copied", 0, probs0T_copied, 6)
            + jobs("attn0_made", 0, attn0_made, 4)
        )
        assert len(RING) % BANKS == 0
        place = {(name, k): at for at, (name, _, _, _, k) in enumerate(RING)}

        def job(name, k):
            return place[name, k]

        def last_reader(i, at):
            it = i
            while True:
                at -= BANKS
                if at < 0:
                    it, at = it - 1, at + len(RING)
                if isinstance(it, int) and it < 0:
                    return None
                _, layer, signal, n, k = RING[at]
                if real(it - layer):
                    return signal, (it - layer) * n + (k + 1)

        def iterations(eng, body):
            body(0, 0)
            body(1, 1)
            with eng.Fori(2, groups, 2) as i:
                body(i, 0)
                body(i + 1, 1)
            body(groups, groups % 2)

        w_names = ["W0", "Wq", "Wk", "Wv", "Wf"]
        w_src_of = {"Wq": Wq, "Wk": Wk, "Wv": Wv, "Wf": Wf}

        block = ctx.enter_context(nc.Block())

        @block.sync
        def _(sp):
            def load_x(i, par):
                if real(i - 2):
                    sp.wait_ge(x2_made, (i - 1) * TILES)
                    sp.sem_inc(sp_passed, 1)
                sp.dma_start(x_in[:, par], x_v[i]).then_inc(x_loaded, 16)
                if real(i - 2):
                    sp.wait_ge(masks_made, 2 * (i - 1))
                    sp.sem_inc(sp_passed, 1)
                sp.dma_start(adj_in[:, par], adj_v[i]).then_inc(adj_loaded[par], 16)

            sp.dma_start(x_in[:, 0], x_v[0]).then_inc(x_loaded, 16)
            wcol = stats[:, 0, 0, 0:3]
            wcol2 = stats[:, 0, 1, 0:3]
            sp.dma_start(wcol, w_dst.rearrange("a e o -> (a e o)").rearrange("(c p) -> p c", p=P), allow_slow_non_contiguous=True).then_inc(consts_loaded, 16)
            sp.dma_start(wcol2, w_src.rearrange("a e o -> (a e o)").rearrange("(c p) -> p c", p=P), allow_slow_non_contiguous=True).then_inc(consts_loaded, 16)
            sp.dma_start(b0_plus1[:], b0.rearrange("(a e) -> a e", a=1).broadcast_to((P, E0))).then_inc(consts_loaded, 16)
            sp.dma_start(bq_col[:], bq.rearrange("(c p) -> p c", p=P), allow_slow_non_contiguous=True).then_inc(consts_loaded, 16)
            sp.dma_start(bk_col[:], bk.rearrange("(c p) -> p c", p=P), allow_slow_non_contiguous=True).then_inc(consts_loaded, 16)
            sp.dma_start(bv_row[:], bv.rearrange("(a e) -> a e", a=1).broadcast_to((P, D))).then_inc(consts_loaded, 16)
            sp.dma_start(bf_row[:], bf.rearrange("(a e) -> a e", a=1).broadcast_to((P, D))).then_inc(consts_loaded, 16)
            sp.dma_start(x2[0:1, 0, :], H_b.rearrange("(a e) -> a e", a=1)).then_inc(consts_loaded, 16)
            sp.dma_start(x2[32:33, 0, :], H_b.rearrange("(a e) -> a e", a=1)).then_inc(consts_loaded, 16)
            sp.dma_start(stage_h[:, 0:3, :], H_w.rearrange("(c p) n -> p c n", p=P)).then_inc(hw_loaded, 16)
            for n, name in enumerate(w_names):
                dst = big[:, 3 * (n % 2):3 * (n % 2) + 3, 0:D]
                if n >= 2:
                    sp.wait_ge(w_low, 3 * (n - 1))
                if name == "W0":
                    for c in range(C):
                        sp.dma_start(dst[:, c, :].rearrange("p (a e) -> p a e", e=E0),
                                     W0[:, c * P:(c + 1) * P, :].rearrange("a p e -> p a e")).then_inc(w_loaded[n % 2], 16)
                else:
                    for c in range(C):
                        sp.dma_start(dst[:, c, :], w_src_of[name][c * P:(c + 1) * P, :]).then_inc(w_loaded[n % 2], 16)
            sp.dma_start(adj_in[:, 0], adj_v[0]).then_inc(adj_loaded[0], 16)

            def body(i, par):
                j = i - 1
                if real(i + 1) and not (isinstance(i, int) and i + 1 >= groups):
                    load_x_guard(i, par)
                if real(i):
                    sp.wait_ge(values0_made, (i + 1) * TILES)
                    if real(i - 1):
                        sp.wait_ge(attn0_full, 2 * i)
                    for g in range(2):
                        sp.dma_start(V0s[64 * g:64 * g + 64], V0[64 - 64 * g:128 - 64 * g]).then_inc(values0_swapped, 16)
                if real(j):
                    sp.wait_ge(values1_made, (j + 1) * TILES)
                    if real(j - 1):
                        sp.wait_ge(attn1_full, 2 * j)
                    for g in range(2):
                        sp.dma_start(V1s[64 * g:64 * g + 64], V1[64 - 64 * g:128 - 64 * g]).then_inc(values1_swapped, 16)
                if real(i):
                    sp.wait_ge(srcdst_copied, i + 1)
                    sp.sem_inc(sp_passed, 1)
                    sp.dma_start(d_scratch[i].rearrange("g h m -> h g m"),
                                 sdT[0:HEADS0, :].rearrange("h (g m) -> h g m", m=N)).then_inc(dst_stored, 16)
                    sp.wait_ge(dst_stored, 16 * (i + 1))
                    sp.sem_inc(sp_passed, 1)
                    if real(i - 1):
                        sp.wait_ge(probs0_turned, 6 * i)
                        sp.sem_inc(sp_passed, 1)
                    for g in range(2):
                        src = d_scratch[i].rearrange("(t g) h m -> g t (h m)", g=2)[g:g + 1]
                        sp.dma_start(z[64 * g:64 * g + 64], src.broadcast_to((64, TILES, HEADS0 * N))).then_inc(dst_spread, 16)
                if real(j):
                    sp.wait_ge(out_made, (j + 1) * TILES)
                    sp.sem_inc(sp_passed, 1)
                    sp.dma_start(out_v[j], ee[:]).then_inc(out_stored, 16)

            def load_x_guard(i, par):
                load_x(i + 1, 1 - par)

            body(0, 0)
            body(1, 1)
            with sp.Fori(2, groups - 2, 2) as i:
                body(i, 0)
                body(i + 1, 1)
            body(groups - 2, 0)
            body(groups - 1, 1)
            body(groups, 0)
            sp.wait_ge(out_stored, 16 * groups)

        @block.gpsimd
        def _(pool):
            pool.memset(ident[:], 0.0).then_inc(zeros_made, 1)
            pool.memset(ident_b[:], 0.0).then_inc(zeros_made, 1)
            pool.memset(wsd[:], 0.0).then_inc(consts_made, 1)
            pool.memset(hb_rows[:].bitcast(F32), 0.0).then_inc(consts_made, 1)
            pool.memset(V0[:, :, :, E0:E0 + 1], 1.0).then_inc(consts_made, 1)
            pool.memset(V1[:, :, :, E1:E1 + 1], 1.0).then_inc(consts_made, 1)
            pool.memset(masked0[:], MASKED0).then_inc(consts_made, 1)
            pool.memset(minus1[:], -1.0).then_inc(consts_made, 1)
            pool.memset(half[:], 0.5).then_inc(consts_made, 1)
            pool.memset(minus_half[:], -0.5).then_inc(consts_made, 1)
            pool.wait_ge(zeros_made, 2)
            for m in (ident, ident_b):
                pool.affine_select(out=m[:], in_=m[:], compare_op=ALU.not_equal, fill=1.0, base=0,
                                   pattern=[[-1, P]], channel_multiplier=1).then_inc(consts_made, 1)
            pool.wait_ge(consts_made, 10)

            def inv_std(layer, g):
                pool.wait_ge((moments0, moments1)[layer], TILES * (g + 1))
                pool.sem_inc(pool_passed, 1)
                pool.tensor_scalar(ve[:, layer], mv[:, layer, :, 1], EPS, None, ALU.add).then_inc((var0_eps, var1_eps)[layer], 1)
                pool.wait_ge((var0_eps, var1_eps)[layer], g + 1)
                if real(g - 1):
                    pool.wait_ge((xn0_made, xn1_made)[layer], TILES * g)
                pool.tensor_tensor(rstd[:, layer], ve[:, layer], minus_half[:], ALU.pow).then_inc((inv_std0, inv_std1)[layer], 1)

            inv_std(0, 0)

            def body(i, par):
                if not real(i):
                    return
                pool.wait_ge(dst_spread, 32 * (i + 1))
                pool.wait_ge(src_copied, i + 1)
                for t in range(TILES):
                    zt = z[:, t].rearrange("p (h m) -> p h m", m=N)
                    pool.tensor_tensor(zt, zt, s_tok[:, t, HEADS0:].unsqueeze(2).broadcast_to((P, HEADS0, N)),
                                       ALU.add).then_inc(scores0_summed, 1)
                if not (isinstance(i, int) and i + 1 >= groups):
                    inv_std(0, i + 1)
                if real(i - 1):
                    pool.wait_ge(out_made, TILES * i)
                for t in range(TILES):
                    pool.wait_ge(gated, TILES * i + t + 1)
                    pool.tensor_tensor(x2[:, t], x_in[:, par, t], ee[:, t], ALU.subtract).then_inc(x2_made, 1)
                inv_std(1, i)
                pool.wait_ge(xn1_made, TILES * (i + 1))
                for t in range(TILES):
                    pool.tensor_tensor(x2[:, t], x2[:, t], bf_row[:], ALU.add).then_inc(x2_biased, 1)

            body(0, 0)
            body(1, 1)
            with pool.Fori(2, groups - 2, 2) as i:
                body(i, 0)
                body(i + 1, 1)
            body(groups - 2, 0)
            body(groups - 1, 1)

        @block.scalar
        def _(act):
            act.wait_ge(consts_loaded, 16 * 9)
            act.wait_ge(consts_made, 10)
            act.wait_ge(hw_turned, 3)
            for c in range(C):
                act.activation(wh["Hw"][:, c, :], ps[:, c, 0:D], ACT.Copy).then_inc(w_high, 1)
            for r in (0, 32):
                act.activation(hb_rows[r:r + 1, :], x2[r:r + 1, 0, :], ACT.Copy).then_inc(rows_made, 1)
            act.activation(ones_rows[:], ident[0:33, :], ACT.Copy, scale=0.0, bias=0.0).then_inc(rows_made, 1)
            act.wait_ge(rows_made, 3)
            act.activation(ones_rows[:], ident[0:33, :], ACT.Identity, scale=0.0, bias=1.0).then_inc(rows_made, 1)
            for n, name in enumerate(w_names):
                act.wait_ge(w_loaded[n % 2], 48 * (n // 2 + 1))
                for c in range(C):
                    act.activation(wh[name][:, c, :], big[:, 3 * (n % 2) + c, 0:D], ACT.Copy).then_inc(w_high, 1)

            def body(i, par):
                j = i - 1
                if real(i):
                    for c in range(C):
                        if c == 0:
                            if real(i - 1):
                                act.wait_ge(gate_full, TILES * i)
                        act.wait_ge(xn0_turned, C * i + c + 1)
                        act.activation(hT0h[:, c], ps[:, job("h0_low", c) % BANKS], ACT.Relu).then_inc(h0_high, 1)
                    for t in range(TILES):
                        act.wait_ge(values0_made, TILES * i + t + 1)
                        if real(i - 1):
                            act.wait_ge(x2_made, TILES * (i - 1) + t + 1)
                        act.activation(ee[:, t], ps[:, job("th_made", t) % BANKS, 0:D], ACT.Tanh).then_inc(th_made, 1)
                        act.wait_ge(gate_full, TILES * i + t + 1)
                        if real(i - 1):
                            act.wait_ge(gated, TILES * (i - 1) + t + 1)
                        act.activation(gate[:, t], ps[:, job("gate_tanh", t) % BANKS, 0:D], ACT.Tanh, scale=0.5).then_inc(gate_tanh, 1)
                    for t in range(TILES):
                        act.wait_ge(gate_tanh, TILES * i + t + 1)
                        act.activation(gate[:, t], gate[:, t], ACT.Identity, scale=0.5, bias=half[:]).then_inc(gate_made, 1)
                if real(j):
                    for c in range(C):
                        if c == 0:
                            if real(j - 1):
                                act.wait_ge(final_full, TILES * j)
                        act.wait_ge(xn1_turned, C * j + c + 1)
                        act.activation(hT1h[:, c], ps[:, job("h1_low", c) % BANKS], ACT.Relu).then_inc(h1_high, 1)
                    act.wait_ge(attn0_full, 2 * (j + 1))
                    for full, copied, name, bias, at in ((q_full, q_copied, "q_copied", bq_col, 0),
                                                         (k_full, k_copied, "k_copied", bk_col, 3)):
                        for c in range(C):
                            act.wait_ge(full, C * j + c + 1)
                            act.activation(big[:, at + c], ps[:, job(name, c) % BANKS], ACT.Identity,
                                           bias=bias[:, c:c + 1]).then_inc(copied, 1)
                if real(i):
                    if real(i - 1):
                        act.wait_ge(srcdst_full, i)
                    if real(i - 2):
                        act.wait_ge(attn1_full, 2 * (i - 1))
                    for c in range(C):
                        act.wait_ge(th_turned, C * i + c + 1)
                        act.activation(thT[:, c], ps[:, job("thT_copied", c) % BANKS], ACT.Copy).then_inc(thT_copied, 1)
                    act.wait_ge(srcdst_full, i + 1)
                    if real(i - 1):
                        act.wait_ge(dst_stored, 16 * i)
                    act.activation(sdT[:], ps[0:2 * HEADS0, job("src_copied", 0) % BANKS], ACT.Copy).then_inc(srcdst_copied, 1)
                if real(j):
                    for t in range(TILES):
                        act.wait_ge(scores1_shifted, 4 * j + 2 * (t // 2) + 2)
                        act.activation(p1[:, t], p1[:, t], ACT.Exp, scale=float(E1) ** -0.5).then_inc(probs1_made, 1)
                    if real(i):
                        act.wait_ge(srcdst_full, i + 1)
                    for c in range(3):
                        act.wait_ge(probs1_turned, 3 * j + c + 1)
                        act.activation(thT[:, c], ps[:, job("probs1T_copied", c) % BANKS], ACT.Copy).then_inc(probs1T_copied, 1)

                def exp0(t):
                    act.wait_ge(scores0_shifted, TILES * i + t + 1)
                    act.activation(z[:, t], z[:, t], ACT.Exp).then_inc(probs0_made, 1)

                if real(i):
                    exp0(0)
                    exp0(1)
                if real(j):
                    act.wait_ge(values1_full, TILES * (j + 1))
                    for c in range(C):
                        act.wait_ge(attn1_turned, C * j + c + 1)
                        act.activation(hT1h[:, c], ps[:, job("attn1_low", c) % BANKS], ACT.Copy).then_inc(attn1_high, 1)
                if real(i):
                    exp0(2)
                    exp0(3)
                    if real(i - 1):
                        act.wait_ge(scores1_full, 2 * i)
                    for q in range(6):
                        act.wait_ge(probs0_turned, 6 * i + q + 1)
                        act.activation(big[:, q], ps[:, job("probs0T_copied", q) % BANKS], ACT.Copy).then_inc(probs0T_copied, 1)
                    if real(i - 1):
                        act.wait_ge(out_stored, 16 * i)
                    for t in range(TILES):
                        act.wait_ge(attn0_made, 4 * i + 2 * (t // 2) + 2)
                        act.activation(ee[:, t], x1[:, t], ACT.Exp, bias=minus1[:]).then_inc(elu_exp, 1)

            iterations(act, body)

        @block.tensor
        def _(pe):
            def turn(dst, src, rows=P):
                return pe.transpose(dst, src, ident[0:rows, 0:rows])

            def take(i, at):
                reader = last_reader(i, at)
                if reader is not None:
                    pe.wait_ge(*reader)
                return ps[:, at % BANKS]

            def product(dst, left_h, left_l, right_h, right_l, more=False):
                for c in range(C):
                    pe.matmul(dst, left_h(c), right_h(c), start=(c == 0), stop=False)
                    pe.matmul(dst, left_h(c), right_l(c), start=False, stop=False)
                    mm = pe.matmul(dst, left_l(c), right_h(c), start=False, stop=(c == C - 1 and not more))
                return mm

            pe.wait_ge(consts_made, 10)
            pe.wait_ge(hw_loaded, 16)
            for c in range(C):
                for f in range(C):
                    mm = turn(ps[:, c, f * P:(f + 1) * P], stage_h[:, f, c * P:(c + 1) * P])
                mm.then_inc(hw_turned, 1)
            pe.wait_ge(small_ready, 5)
            pe.wait_ge(rows_made, 4)
            pe.wait_ge(w_low, 15)

            def turn_tokens(name, done, src, i, g):
                for c in range(C):
                    take(i, job(name, c))
                    for t in range(TILES):
                        mm = turn(ps[:, job(name, c) % BANKS, t * P:(t + 1) * P], src(t, c))
                    mm.then_inc(done, 1)

            def body(i, par):
                j = i - 1
                if real(i):
                    pe.wait_ge(xn0_made, TILES * (i + 1))
                    turn_tokens("h0_low", xn0_turned, lambda t, c: xn0[:, par, t, c * P:(c + 1) * P], i, i)
                    pe.wait_ge(h0_low, C * (i + 1))
                    for t in range(TILES):
                        toks = slice(t * P, (t + 1) * P)
                        take(i, job("th_made", t))
                        product(ps[:, job("th_made", t) % BANKS, 0:D], lambda c: hT0h[:, c, toks], lambda c: hT0l[:, c, toks],
                                lambda c: wh["W0"][:, c], lambda c: wl["W0"][:, c]).then_inc(values0_full, 1)
                        take(i, job("gate_tanh", t))
                        dst = ps[:, job("gate_tanh", t) % BANKS, 0:D]
                        product(dst, lambda c: hT0h[:, c, toks], lambda c: hT0l[:, c, toks],
                                lambda c: wh["Hw"][:, c], lambda c: wl["Hw"][:, c], more=True)
                        pe.matmul(dst, ones_rows[:], hb_rows[:], start=False, stop=True).then_inc(gate_full, 1)
                if real(j):
                    pe.wait_ge(xn1_made, TILES * (j + 1))
                    turn_tokens("h1_low", xn1_turned, lambda t, c: p1[:, t, c * P:(c + 1) * P], i, j)
                    pe.wait_ge(h1_low, C * (j + 1))
                    for full, name, w in ((q_full, "q_copied", "Wq"), (k_full, "k_copied", "Wk")):
                        for o in range(C):
                            take(i, job(name, o))
                            cols = slice(o * P, (o + 1) * P)
                            product(ps[:, job(name, o) % BANKS], lambda c: wh[w][:, c, cols], lambda c: wl[w][:, c, cols],
                                    lambda c: hT1h[:, c], lambda c: hT1l[:, c]).then_inc(full, 1)
                    for t in range(TILES):
                        toks = slice(t * P, (t + 1) * P)
                        take(i, job("values1_made", t))
                        product(ps[:, job("values1_made", t) % BANKS, 0:D], lambda c: hT1h[:, c, toks], lambda c: hT1l[:, c, toks],
                                lambda c: wh["Wv"][:, c], lambda c: wl["Wv"][:, c]).then_inc(values1_full, 1)
                if real(i):
                    pe.wait_ge(th_made, TILES * (i + 1))
                    turn_tokens("thT_copied", th_turned, lambda t, c: ee[:, t, c * P:(c + 1) * P], i, i)
                    pe.wait_ge(thT_copied, C * (i + 1))
                    take(i, job("src_copied", 0))
                    for c in range(C):
                        mm = pe.matmul(ps[0:2 * HEADS0, job("src_copied", 0) % BANKS], wsd[:, c], thT[:, c],
                                       start=(c == 0), stop=(c == C - 1))
                    mm.then_inc(srcdst_full, 1)

                def scores(pair):
                    tiles = slice(2 * pair, 2 * pair + 2)
                    banks = []
                    for odd in range(2):
                        take(i, job("scores1_shifted", 2 * pair + odd))
                        bank = ps[:, job("scores1_shifted", 2 * pair + odd) % BANKS, 0:D].rearrange("p (t h m) -> p t h m", t=2, m=N)
                        pe.matmul(bank, ident_b[:], mask1[:, tiles].unsqueeze(2).broadcast_to((P, 2, PAIRS1, N)),
                                  start=True, stop=False, skip_group_check=True)
                        banks.append(bank)
                    for t in range(2):
                        for h in range(HEADS1):
                            r = 64 * (h % 2)
                            for g in range(2):
                                at = (2 * pair + t) * P + g * N
                                mm = pe.matmul(banks[h % 2][g * N:(g + 1) * N, t, h // 2], big[r:r + E1, h // 2, at:at + N],
                                               big[r:r + E1, 3 + h // 2, at:at + N], start=False, stop=True,
                                               skip_group_check=True)
                    mm.then_inc(scores1_full, 1)

                if real(j):
                    pe.wait_ge(q_copied, C * (j + 1))
                    pe.wait_ge(k_copied, C * (j + 1))
                    pe.wait_ge(masks_made, 2 * (j + 1))
                    scores(0)
                if real(i):
                    pe.wait_ge(srcdst_copied, i + 1)
                    pe.sem_inc(pe_passed, 1)
                    for t in range(TILES):
                        mm = turn(ps[:, job("src_copied", 0) % BANKS, t * 2 * HEADS0:(t + 1) * 2 * HEADS0],
                                  sdT[:, t * P:(t + 1) * P], 2 * HEADS0)
                    mm.then_inc(srcdst_turned, 1)

                def turn_probs(name, ready, done, src, pairs, g, jobs):
                    for q in range(jobs):
                        take(i, job(name, q))
                        for k in range(4):
                            t, pair = divmod(4 * q + k, pairs)
                            if k == 0 or pair == 0:
                                pe.wait_ge(ready, TILES * g + t + 1)
                            mm = turn(ps[:, job(name, q) % BANKS, k * P:(k + 1) * P], src[:, t, pair * P:(pair + 1) * P])
                        mm.then_inc(done, 1)

                def attend(pair, name, done, ready, swapped, probsT, V, Vs, heads, width, g_, ready_n):
                    pairs = heads // 2
                    last = ((2 * pair + 2) * pairs - 1) // 4
                    pe.wait_ge(swapped, 32 * (g_ + 1))
                    pe.sem_inc(pe_passed, 1)
                    pe.wait_ge(ready, ready_n * g_ + last + 1)
                    pe.sem_inc(pe_passed, 1)
                    for odd in range(2):
                        take(i, job(name, 2 * pair + odd))
                        pe.sem_inc(pe_passed, 1)
                    banks = [ps[:, job(name, 2 * pair + odd) % BANKS, 0:heads * (width + 1)]
                             .rearrange("p (t h e) -> p t h e", t=2, e=width + 1) for odd in range(2)]
                    for t in range(2 * pair, 2 * pair + 2):
                        for h in range(heads):
                            q, k = divmod(t * pairs + h // 2, 4)
                            r = 64 * (h % 2)
                            for g in range(2):
                                vals = V if h % 2 == g else Vs
                                mm = pe.matmul(banks[h % 2][g * N:(g + 1) * N, t % 2, h // 2],
                                               probsT[r:r + N, q, k * P + g * N:k * P + (g + 1) * N],
                                               vals[r:r + N, t, h], start=True, stop=True, skip_group_check=True)
                    mm.then_inc(done, 1)

                if real(j):
                    scores(1)
                    turn_probs("probs1T_copied", probs1_made, probs1_turned, p1, PAIRS1, j, 3)
                    for pair in range(2):
                        attend(pair, "attn1_made", attn1_full, probs1T_copied, values1_swapped, thT, V1, V1s, HEADS1, E1, j, 3)
                    pe.wait_ge(attn1_made, TILES * (j + 1))
                    turn_tokens("attn1_low", attn1_turned, lambda t, c: x1[:, t, c * P:(c + 1) * P], i, j)
                    pe.wait_ge(attn1_low, C * (j + 1))
                    for t in range(TILES):
                        toks = slice(t * P, (t + 1) * P)
                        take(i, job("out_made", t))
                        product(ps[:, job("out_made", t) % BANKS, 0:D], lambda c: hT1h[:, c, toks], lambda c: hT1l[:, c, toks],
                                lambda c: wh["Wf"][:, c], lambda c: wl["Wf"][:, c]).then_inc(final_full, 1)
                if real(i):
                    turn_probs("probs0T_copied", probs0_made, probs0_turned, z, PAIRS0, i, 6)
                    for pair in range(2):
                        attend(pair, "attn0_made", attn0_full, probs0T_copied, values0_swapped, big, V0, V0s, HEADS0, E0, i, 6)

            iterations(pe, body)

        @block.vector
        def _(dve):
            dve.wait_ge(consts_loaded, 16 * 9)
            dve.wait_ge(consts_made, 10)
            for k, col in ((0, stats[:, 0, 0, 0:3]), (HEADS0, stats[:, 0, 1, 0:3])):
                for q in range(4):
                    rows = slice(32 * q, 32 * q + 32)
                    for c in range(C):
                        at = k + 4 * c + q
                        dve.tensor_copy(wsd[rows, c, at:at + 1], col[rows, c:c + 1])
            dve.tensor_scalar(b0_plus1[:], b0_plus1[:], 1.0, None, ALU.add).then_inc(small_ready, 1)
            for c in range(C):
                dve.wait_ge(w_high, c + 1)
                dve.tensor_tensor(wl["Hw"][:, c, :], ps[:, c, 0:D], wh["Hw"][:, c, :].bitcast(F32), ALU.subtract)\
                    .then_inc(small_ready, 1)
            dve.wait_ge(rows_made, 2)
            dve.tensor_tensor(hb_rows[32:33, :], x2[32:33, 0, :], hb_rows[32:33, :].bitcast(F32), ALU.subtract)\
                .then_inc(small_ready, 1)
            for n, name in enumerate(w_names):
                for c in range(C):
                    dve.wait_ge(w_high, 3 * (n + 1) + c + 1)
                    dve.tensor_tensor(wl[name][:, c, :], big[:, 3 * (n % 2) + c, 0:D], wh[name][:, c, :].bitcast(F32),
                                      ALU.subtract).then_inc(w_low, 1)

            def row_stats(layer, src, t, g):
                dve.bn_stats(stats[:, layer, t], src).then_inc((stats0, stats1)[layer], 1)

            def row_sums(layer, g):
                for t in range(TILES):
                    dve.wait_ge((stats0, stats1)[layer], TILES * g + t + 1)
                    dve.sem_inc(dve_passed, 1)
                    dve.bn_aggr(mv[:, layer, t], stats[:, layer, t]).then_inc((moments0, moments1)[layer], 1)

            def normalise(layer, src, dst, done, g):
                dve.wait_ge((inv_std0, inv_std1)[layer], g + 1)
                for t in range(TILES):
                    dve.tensor_scalar(dst(t), src(t), mv[:, layer, t, 0:1], rstd[:, layer, t:t + 1],
                                      ALU.subtract, ALU.mult).then_inc(done, 1)

            def norm0(g, par):
                dve.wait_ge(x_loaded, 16 * (g + 1))
                for t in range(TILES):
                    row_stats(0, x_in[:, par, t], t, g)
                row_sums(0, g)

            def norm0_end(g, par):
                normalise(0, lambda t: x_in[:, par, t], lambda t: xn0[:, par, t], xn0_made, g)

            dve.wait_ge(small_ready, 5)
            norm0(0, 0)
            norm0_end(0, 0)

            def body(i, par):
                j = i - 1
                if real(i):
                    for c in range(C):
                        dve.wait_ge(h0_high, C * i + c + 1)
                        dve.scalar_tensor_tensor(hT0l[:, c], ps[:, job("h0_low", c) % BANKS], 0.0, hT0h[:, c].bitcast(F32),
                                                 ALU.max, ALU.subtract).then_inc(h0_low, 1)
                    if real(i - 1):
                        dve.wait_ge(values0_swapped, 32 * i)
                    for t in range(TILES):
                        dve.wait_ge(values0_full, TILES * i + t + 1)
                        if real(i - 1):
                            dve.wait_ge(attn0_full, 2 * (i - 1) + t // 2 + 1)
                        dve.tensor_tensor(V0[:, t, :, 0:E0], ps[:, job("th_made", t) % BANKS, 0:D].rearrange("p (h e) -> p h e", e=E0),
                                          b0_plus1[:].unsqueeze(1).broadcast_to((P, HEADS0, E0)), ALU.add)\
                            .then_inc(values0_made, 1)
                if real(j):
                    for c in range(C):
                        dve.wait_ge(h1_high, C * j + c + 1)
                        dve.scalar_tensor_tensor(hT1l[:, c], ps[:, job("h1_low", c) % BANKS], 0.0, hT1h[:, c].bitcast(F32),
                                                 ALU.max, ALU.subtract).then_inc(h1_low, 1)
                    if real(j - 1):
                        dve.wait_ge(attn1_full, 2 * j)
                    if real(j - 1):
                        dve.wait_ge(values1_swapped, 32 * j)
                    for t in range(TILES):
                        dve.wait_ge(values1_full, TILES * j + t + 1)
                        dve.tensor_tensor(V1[:, t, :, 0:E1], ps[:, job("values1_made", t) % BANKS, 0:D].rearrange("p (h e) -> p h e", e=E1),
                                          bv_row[:].rearrange("p (h e) -> p h e", e=E1), ALU.add).then_inc(values1_made, 1)

                def shift1(pair, odd):
                    n = 4 * j + 2 * pair + odd + 1
                    tiles = slice(2 * pair, 2 * pair + 2)
                    bank = ps[:, job("scores1_shifted", 2 * pair + odd) % BANKS, 0:D].rearrange("p (t h m) -> p t h m", t=2, m=N)
                    top = mx1[:, tiles].rearrange("p t (h o) -> p t h o", o=2)[:, :, :, odd]
                    dve.wait_ge(scores1_full, 2 * j + pair + 1)
                    dve.tensor_reduce(top, bank, AX_X, ALU.max).then_inc(max1_made, 1)
                    dve.wait_ge(max1_made, n)
                    dve.tensor_tensor(p1[:, tiles].rearrange("p t (h o m) -> p t h o m", o=2, m=N)[:, :, :, odd], bank,
                                      top.unsqueeze(3).broadcast_to((P, 2, PAIRS1, N)), ALU.subtract)\
                        .then_inc(scores1_shifted, 1)

                if real(j):
                    shift1(0, 0)
                    shift1(0, 1)
                if real(i):
                    dve.wait_ge(srcdst_turned, i + 1)
                    if real(i - 1):
                        dve.wait_ge(scores0_summed, TILES * i)
                    dve.tensor_copy(s_tok[:].rearrange("p t h -> p (t h)"),
                                    ps[:, job("src_copied", 0) % BANKS, 0:TILES * 2 * HEADS0]).then_inc(src_copied, 1)
                if real(j):
                    shift1(1, 0)
                    shift1(1, 1)
                if real(i):
                    dve.wait_ge(adj_loaded[par], 8 * (i - par) + 16)
                    if real(i - 1):
                        dve.wait_ge(masked, TILES * i)
                    dve.tensor_scalar(not_adj[:], adj_in[:, par], 0.0, None, ALU.is_equal).then_inc(masks_made, 1)
                    if real(i - 1):
                        dve.wait_ge(scores1_full, 2 * i)
                    dve.tensor_scalar(mask1[:], adj_in[:, par], -1.0, MASKED1 * float(E1) ** 0.5, ALU.add, ALU.mult)\
                        .then_inc(masks_made, 1)

                def softmax0(t):
                    n = TILES * i + t + 1
                    zt = z[:, t].rearrange("p (h m) -> p h m", m=N)
                    dve.wait_ge(scores0_summed, n)
                    dve.scalar_tensor_tensor(z[:, t], z[:, t], SLOPE, z[:, t], ALU.mult, ALU.max).then_inc(leaky_made, 1)
                    dve.wait_ge(leaky_made, n)
                    dve.sem_inc(dve_passed, 1)
                    dve.wait_ge(masks_made, 2 * (i + 1))
                    dve.sem_inc(dve_passed, 1)
                    dve.copy_predicated(zt, not_adj[:, t].unsqueeze(1).broadcast_to((P, HEADS0, N)),
                                        masked0[:].unsqueeze(2).broadcast_to((P, HEADS0, N))).then_inc(masked, 1)
                    dve.wait_ge(masked, n)
                    dve.tensor_reduce(mx0[:, t], zt, AX_X, ALU.max).then_inc(max0_made, 1)
                    dve.wait_ge(max0_made, n)
                    dve.tensor_tensor(zt, zt, mx0[:, t].unsqueeze(2).broadcast_to((P, HEADS0, N)), ALU.subtract)\
                        .then_inc(scores0_shifted, 1)

                def divide(u, name, full, dst, sums, inverted, done, heads, width, g):
                    pair, odd = divmod(u, 2)
                    tiles = slice(2 * pair, 2 * pair + 2)
                    v = ps[:, job(name, u) % BANKS, 0:heads * (width + 1)].rearrange("p (t h e) -> p t h e", t=2, e=width + 1)
                    inv = sums[:, tiles].rearrange("p t (h o) -> p t h o", o=2)[:, :, :, odd]
                    dve.wait_ge(full, 2 * g + pair + 1)
                    dve.reciprocal(inv, v[:, :, :, width]).then_inc(inverted, 1)
                    dve.wait_ge(inverted, 4 * g + u + 1)
                    dve.tensor_tensor(dst[:, tiles].rearrange("p t (h o e) -> p t h o e", o=2, e=width)[:, :, :, odd],
                                      v[:, :, :, 0:width], inv.unsqueeze(3).broadcast_to((P, 2, heads // 2, width)),
                                      ALU.mult).then_inc(done, 1)

                if real(i):
                    softmax0(0)
                    softmax0(1)
                if real(j):
                    for u in range(4):
                        divide(u, "attn1_made", attn1_full, x1, rs1, inv1_made, attn1_made, HEADS1, E1, j)
                    for c in range(C):
                        dve.wait_ge(attn1_high, C * j + c + 1)
                        dve.tensor_tensor(hT1l[:, c], ps[:, job("attn1_low", c) % BANKS], hT1h[:, c].bitcast(F32), ALU.subtract)\
                            .then_inc(attn1_low, 1)
                if real(i):
                    softmax0(2)
                    softmax0(3)
                if real(j):
                    dve.wait_ge(x2_biased, TILES * (j + 1))
                    if real(i):
                        dve.wait_ge(th_turned, C * (i + 1))
                    for t in range(TILES):
                        dve.wait_ge(final_full, TILES * j + t + 1)
                        dve.tensor_tensor(ee[:, t], ps[:, job("out_made", t) % BANKS, 0:D], x2[:, t], ALU.add).then_inc(out_made, 1)
                more = real(i) and not (isinstance(i, int) and i + 1 >= groups)
                if more:
                    norm0(i + 1, 1 - par)

                def close(t):
                    n = TILES * i + t + 1
                    dve.wait_ge(elu_exp, n)
                    dve.scalar_tensor_tensor(ee[:, t], ee[:, t], 1.0, x1[:, t], ALU.min, ALU.max).then_inc(elu_made, 1)
                    dve.scalar_tensor_tensor(x_in[:, par, t], xn0[:, par, t], 0.0, x_in[:, par, t], ALU.max, ALU.add)\
                        .then_inc(x_plus_h, 1)
                    dve.wait_ge(elu_made, n)
                    dve.scalar_tensor_tensor(x1[:, t], xn0[:, par, t], 0.0, ee[:, t], ALU.max, ALU.subtract)\
                        .then_inc(h_less_elu, 1)
                    dve.wait_ge(h_less_elu, n)
                    dve.wait_ge(x_plus_h, n)
                    dve.wait_ge(gate_made, n)
                    dve.scalar_tensor_tensor(ee[:, t], x1[:, t], 1.0, gate[:, t], ALU.add, ALU.mult).then_inc(gated, 1)

                if real(i):
                    if real(i - 1):
                        dve.wait_ge(attn1_turned, C * i)
                    for t in range(TILES + 2):
                        if t % 2 == 0 and t < TILES:
                            divide(t, "attn0_made", attn0_full, x1, rs0, inv0_made, attn0_made, HEADS0, E0, i)
                            divide(t + 1, "attn0_made", attn0_full, x1, rs0, inv0_made, attn0_made, HEADS0, E0, i)
                        if t == 0 and more:
                            norm0_end(i + 1, 1 - par)
                        if 1 <= t <= TILES:
                            close(t - 1)
                        if t >= 2:
                            dve.wait_ge(x2_made, TILES * i + t - 1)
                            row_stats(1, x2[:, t - 2], t - 2, i)
                    row_sums(1, i)
                    if real(i - 1):
                        dve.wait_ge(probs1_turned, 3 * i)
                    normalise(1, lambda t: x2[:, t], lambda t: p1[:, t], xn1_made, i)

            body(0, 0)
            body(1, 1)
            with dve.Fori(2, groups - 2, 2) as i:
                body(i, 0)
                body(i + 1, 1)
            body(groups - 2, 0)
            body(groups - 1, 1)
            body(groups, 0)


_INS = ['x', 'adj', 'L0_gnn_W', 'L0_gnn_b', 'L0_gnn_w_src', 'L0_gnn_w_dst', 'L0_gnn_H_w', 'L0_gnn_H_b', 'L1_gnn_Wq',
        'L1_gnn_bq', 'L1_gnn_Wk', 'L1_gnn_bk', 'L1_gnn_Wv', 'L1_gnn_bv', 'L1_gnn_Wf', 'L1_gnn_bf']


def kernel(**inputs):
    import concourse.bacc as _bacc
    from concourse.bass_utils import run_bass_kernel_spmd as _run

    nc = _bacc.Bacc("TRN2", target_bir_lowering=False, num_devices=1)
    arrays, args = {}, []
    for name in _INS:
        a = np.ascontiguousarray(inputs[name])
        arrays[f"in_{name}_dram"] = a
        args.append(nc.dram_tensor(f"in_{name}_dram", a.shape, mybir.dt.from_np(a.dtype), kind="ExternalInput").ap())
    shape = np.shape(inputs['x'])
    graphs = 2 * TILES
    out = nc.dram_tensor("out_0_dram", shape, F32, kind="ExternalOutput").ap()
    scratch = nc.dram_tensor("d_scratch", (shape[0] // graphs, graphs, HEADS0, N), F32, kind="Internal").ap()
    two_layer_gnn(nc, *args, out, scratch)
    r = _run(nc, [arrays], core_ids=[0])
    return r.results[0]["out_0_dram"]
```

```python
from contextlib import ExitStack

import numpy as np

import concourse.bass as bass
from concourse import mybir

ACT = mybir.ActivationFunctionType
ALU = mybir.AluOpType
AX_X = mybir.AxisListType.X
F32 = mybir.dt.float32
F32R = mybir.dt.float32r
BF16 = mybir.dt.bfloat16
U8 = mybir.dt.uint8

P = 128
N = 64
D = 384
C = D // P
TILES = 4
TOK = TILES * P
HEADS0, E0 = 12, 32
HEADS1, E1 = 6, 64
PAIRS0, PAIRS1 = HEADS0 // 2, HEADS1 // 2
BANKS = 8
SLOPE = 0.2
MASKED0 = -999.0
MASKED1 = 9e15
EPS = 1e-5

def two_layer_gnn(nc, x, adj, W0, b0, w_src, w_dst, H_w, H_b, Wq, bq, Wk, bk, Wv, bv, Wf, bf, out, d_scratch):
    groups = x.shape[0] * x.shape[1] // TOK
    x_v = x.rearrange("a n d -> (a n) d").rearrange("(i t p) d -> i p t d", t=TILES, p=P)
    out_v = out.rearrange("a n d -> (a n) d").rearrange("(i t p) d -> i p t d", t=TILES, p=P)
    adj_v = adj.rearrange("a n m -> (a n) m").rearrange("(i t p) m -> i p t m", t=TILES, p=P)

    with ExitStack() as ctx:
        def sb(name, shape, dt=F32):
            return ctx.enter_context(nc.sbuf_tensor(name, shape, dt))

        def sem(name):
            return ctx.enter_context(nc.semaphore(name))

        wh = {k: sb(f"{k}_hi", [P, C, D], F32R) for k in ("W0", "Hw", "Wq", "Wk", "Wv", "Wf")}
        wl = {k: sb(f"{k}_lo", [P, C, D], F32R) for k in ("W0", "Hw", "Wq", "Wk", "Wv", "Wf")}
        wsd = sb("wsd", [P, C, 2 * HEADS0])
        hb_rows = sb("hb_rows", [33, D], F32R)
        ones_rows = sb("ones_rows", [33, P], F32R)
        b0_plus1 = sb("b0_plus1", [P, E0])
        bq_col = sb("bq_col", [P, C])
        bk_col = sb("bk_col", [P, C])
        bv_row = sb("bv_row", [P, D])
        bf_row = sb("bf_row", [P, D])
        ident = sb("ident", [P, P])
        ident_b = sb("ident_b", [P, P], BF16)
        masked0 = sb("masked0", [P, 1])
        minus1 = sb("minus1", [P, 1])
        half = sb("half", [P, 1])
        minus_half = sb("minus_half", [P, TILES])

        x_in = sb("x_in", [P, 2, TILES, D])
        xn0 = sb("xn0", [P, 2, TILES, D])
        adj_in = sb("adj_in", [P, 2, TILES, N], U8)
        hT0h = sb("hT0h", [P, C, TOK], F32R)
        hT0l = sb("hT0l", [P, C, TOK], F32R)
        hT1h = sb("hT1h", [P, C, TOK], F32R)
        hT1l = sb("hT1l", [P, C, TOK], F32R)
        gate = sb("gate", [P, TILES, D])
        V0 = sb("V0", [P, TILES, HEADS0, E0 + 1])
        V0s = sb("V0s", [P, TILES, HEADS0, E0 + 1])
        thT = sb("thT", [P, C, TOK])
        sdT = sb("sdT", [2 * HEADS0, TOK])
        s_tok = sb("s_tok", [P, TILES, 2 * HEADS0])
        z = sb("z", [P, TILES, HEADS0 * N])
        big = sb("big", [P, 6, TOK])
        x1 = sb("x1", [P, TILES, D])
        ee = sb("ee", [P, TILES, D])
        x2 = sb("x2", [P, TILES, D])
        V1 = sb("V1", [P, TILES, HEADS1, E1 + 1])
        V1s = sb("V1s", [P, TILES, HEADS1, E1 + 1])
        p1 = sb("p1", [P, TILES, D])
        not_adj = sb("not_adj", [P, TILES, N], U8)
        mask1 = sb("mask1", [P, TILES, N], BF16)
        mx0 = sb("mx0", [P, TILES, HEADS0])
        rs0 = sb("rs0", [P, TILES, HEADS0])
        mx1 = sb("mx1", [P, TILES, HEADS1])
        rs1 = sb("rs1", [P, TILES, HEADS1])
        stats = sb("stats", [P, 2, TILES, 6])
        mv = sb("mv", [P, 2, TILES, 2])
        ve = sb("ve", [P, 2, TILES])
        rstd = sb("rstd", [P, 2, TILES])
        ps = ctx.enter_context(nc.psum_tensor("ps", [P, BANKS, 512], F32))
        staged = {"Hw": x1[:, 0:3], "W0": big[:, 0:3, 0:D], "Wq": big[:, 3:6, 0:D], 
                  "Wk": z[:, 0:2].rearrange("p t m -> p (t m)")[:, 0:C * D].rearrange("p (c d) -> p c d", d=D),
                  "Wv": z[:, 2:4].rearrange("p t m -> p (t m)")[:, 0:C * D].rearrange("p (c d) -> p c d", d=D),
                  "Wf": p1[:, 0:3]}

        hw_loaded = sem("hw_loaded")
        consts_loaded = sem("consts_loaded")
        consts_made = sem("consts_made")
        small_ready = sem("small_ready")
        w_high = sem("w_high")
        w_low = sem("w_low")
        hw_turned = sem("hw_turned")
        zeros_made = sem("zeros_made")
        rows_made = sem("rows_made")
        w_loaded = {k: sem(f"{k}_loaded") for k in ("W0", "Wq", "Wk", "Wv", "Wf")}
        w0_high = sem("w0_high")
        w0_low = sem("w0_low")
        x_loaded = [sem("x_loaded_0"), sem("x_loaded_1")]
        values0_swapped = sem("values0_swapped")
        values1_swapped = sem("values1_swapped")
        dst_stored = sem("dst_stored")
        dst_spread = sem("dst_spread")
        out_stored = sem("out_stored")
        adj_loaded = [sem("adj_loaded_0"), sem("adj_loaded_1")]
        xn0_turned = sem("xn0_turned")
        values0_full = sem("values0_full")
        gate_full = sem("gate_full")
        xn1_turned = sem("xn1_turned")
        q_full = sem("q_full")
        k_full = sem("k_full")
        values1_full = sem("values1_full")
        th_turned = sem("th_turned")
        srcdst_full = sem("srcdst_full")
        srcdst_turned = sem("srcdst_turned")
        scores1_full = sem("scores1_full")
        probs1_turned = sem("probs1_turned")
        attn1_full = sem("attn1_full")
        attn1_turned = sem("attn1_turned")
        final_full = sem("final_full")
        probs0_turned = sem("probs0_turned")
        attn0_full = sem("attn0_full")
        h0_high = sem("h0_high")
        th_made = sem("th_made")
        gate_tanh = sem("gate_tanh")
        gate_made = sem("gate_made")
        h1_high = sem("h1_high")
        q_copied = sem("q_copied")
        k_copied = sem("k_copied")
        thT_copied = sem("thT_copied")
        srcdst_copied = sem("srcdst_copied")
        probs1_made = sem("probs1_made")
        probs1T_copied = sem("probs1T_copied")
        attn1_high = sem("attn1_high")
        probs0_made = sem("probs0_made")
        probs0T_copied = sem("probs0T_copied")
        elu_exp = sem("elu_exp")
        stats0 = sem("stats0")
        moments0 = sem("moments0")
        xn0_made = sem("xn0_made")
        h0_low = sem("h0_low")
        values0_made = sem("values0_made")
        h1_low = sem("h1_low")
        values1_made = sem("values1_made")
        src_copied = sem("src_copied")
        max1_made = sem("max1_made")
        scores1_shifted = sem("scores1_shifted")
        not_adj_made = sem("not_adj_made")
        mask1_made = sem("mask1_made")
        leaky_made = sem("leaky_made")
        masked = sem("masked")
        max0_made = sem("max0_made")
        scores0_shifted = sem("scores0_shifted")
        inv1_made = sem("inv1_made")
        attn1_made = sem("attn1_made")
        attn1_low = sem("attn1_low")
        out_made = sem("out_made")
        inv0_made = sem("inv0_made")
        attn0_made = sem("attn0_made")
        elu_made = sem("elu_made")
        h_less_elu = sem("h_less_elu")
        x_plus_h = sem("x_plus_h")
        gated = sem("gated")
        stats1 = sem("stats1")
        moments1 = sem("moments1")
        xn1_made = sem("xn1_made")
        scores0_summed = sem("scores0_summed")
        var0_eps = sem("var0_eps")
        inv_std0 = sem("inv_std0")
        x2_made = sem("x2_made")
        var1_eps = sem("var1_eps")
        inv_std1 = sem("inv_std1")
        x2_biased = sem("x2_biased")
        sp_passed = sem("sp_passed")
        pool_passed = sem("pool_passed")
        pe_passed = sem("pe_passed")
        dve_passed = sem("dve_passed")

        def real(g):
            return not isinstance(g, int) or 0 <= g < groups

        def jobs(name, layer, signal, n):
            return [(name, layer, signal, n, k) for k in range(n)]

        pairs_of_jobs = zip(jobs("th_made", 0, th_made, 4), jobs("gate_tanh", 0, gate_tanh, 4))
        NEXT = -1
        RING = (
            [x for pair in pairs_of_jobs for x in pair]
            + jobs("h1_low", 1, h1_low, 3)
            + jobs("thT_copied", 0, thT_copied, 3)
            + jobs("q_copied", 1, q_copied, 3)[0:1]
            + jobs("src_copied", 0, src_copied, 1)
            + jobs("q_copied", 1, q_copied, 3)[1:3]
            + jobs("k_copied", 1, k_copied, 3)
            + jobs("values1_made", 1, values1_made, 4)
            + jobs("scores1_shifted", 1, scores1_shifted, 4)
            + jobs("h0_low", NEXT, h0_low, 3)
            + jobs("probs1T_copied", 1, probs1T_copied, 3)
            + jobs("attn1_made", 1, attn1_made, 4)
            + jobs("probs0T_copied", 0, probs0T_copied, 6)
            + jobs("attn0_made", 0, attn0_made, 4)[0:2]
            + jobs("attn1_low", 1, attn1_low, 3)
            + jobs("attn0_made", 0, attn0_made, 4)[2:4]
            + jobs("out_made", 1, out_made, 4)
        )
        assert len(RING) % BANKS == 0
        place = {(name, k): at for at, (name, _, _, _, k) in enumerate(RING)}

        def job(name, k):
            return place[name, k]

        def last_reader(i, at):
            it = i
            while True:
                at -= BANKS
                if at < 0:
                    it, at = it - 1, at + len(RING)
                if isinstance(it, int) and it < NEXT:
                    return None
                _, layer, signal, n, k = RING[at]
                if real(it - layer):
                    return signal, (it - layer) * n + (k + 1)

        def iterations(eng, body):
            body(0, 0)
            body(1, 1)
            with eng.Fori(2, groups - 2, 2) as i:
                body(i, 0)
                body(i + 1, 1)
            body(groups - 2, 0)
            body(groups - 1, 1)
            body(groups, 0)

        w_late = ["Wq", "Wk", "Wv", "Wf"]
        w_source = {"Wq": Wq, "Wk": Wk, "Wv": Wv, "Wf": Wf}

        wcol, wcol2 = stats[:, 1, 0, 0:C], stats[:, 1, 1, 0:C]

        block = ctx.enter_context(nc.Block())

        @block.sync
        def _(sp):
            def load_x(i, par):
                if real(i - 2):
                    sp.wait_ge(x2_made, (i - 1) * TILES)
                    sp.sem_inc(sp_passed, 1)
                sp.dma_start(x_in[:, par], x_v[i]).then_inc(x_loaded[par], 16)
                if real(i - 2):
                    sp.wait_ge(mask1_made, i - 1)
                    sp.sem_inc(sp_passed, 1)
                sp.dma_start(adj_in[:, par], adj_v[i]).then_inc(adj_loaded[par], 16)

            sp.dma_start(x_in[:, 0], x_v[0]).then_inc(x_loaded[0], 16)
            sp.dma_start(staged["Hw"], H_w.rearrange("(c p) n -> p c n", p=P)).then_inc(hw_loaded, 16)
            for c in range(C):
                sp.dma_start(staged["W0"][:, c, :].rearrange("p (a e) -> p a e", e=E0),
                             W0[:, c * P:(c + 1) * P, :].rearrange("a p e -> p a e")).then_inc(w_loaded["W0"], 16)
            sp.dma_start(b0_plus1[:], b0.rearrange("(a e) -> a e", a=1).broadcast_to((P, E0))).then_inc(consts_loaded, 16)
            sp.dma_start(x2[0:1, 0, :], H_b.rearrange("(a e) -> a e", a=1)).then_inc(consts_loaded, 16)
            sp.dma_start(x2[32:33, 0, :], H_b.rearrange("(a e) -> a e", a=1)).then_inc(consts_loaded, 16)
            sp.dma_start(wcol, w_dst.rearrange("a e o -> (a e o)").rearrange("(c p) -> p c", p=P), allow_slow_non_contiguous=True).then_inc(consts_loaded, 16)
            sp.dma_start(wcol2, w_src.rearrange("a e o -> (a e o)").rearrange("(c p) -> p c", p=P), allow_slow_non_contiguous=True).then_inc(consts_loaded, 16)
            sp.dma_start(bq_col[:], bq.rearrange("(c p) -> p c", p=P), allow_slow_non_contiguous=True).then_inc(consts_loaded, 16)
            sp.dma_start(bk_col[:], bk.rearrange("(c p) -> p c", p=P), allow_slow_non_contiguous=True).then_inc(consts_loaded, 16)
            sp.dma_start(bv_row[:], bv.rearrange("(a e) -> a e", a=1).broadcast_to((P, D))).then_inc(consts_loaded, 16)
            sp.dma_start(bf_row[:], bf.rearrange("(a e) -> a e", a=1).broadcast_to((P, D))).then_inc(consts_loaded, 16)
            sp.dma_start(adj_in[:, 0], adj_v[0]).then_inc(adj_loaded[0], 16)
            for name in w_late:
                sp.dma_start(staged[name], w_source[name].rearrange("(c p) n -> p c n", p=P)).then_inc(w_loaded[name], 16)

            def body(i, par):
                j = i - 1
                if real(i + 1):
                    load_x(i + 1, 1 - par)
                if real(i):
                    sp.wait_ge(values0_made, (i + 1) * TILES)
                    sp.sem_inc(sp_passed, 1)
                    if real(i - 1):
                        sp.wait_ge(attn0_full, 2 * i)
                        sp.sem_inc(sp_passed, 1)
                    for g in range(2):
                        sp.dma_start(V0s[64 * g:64 * g + 64], V0[64 - 64 * g:128 - 64 * g]).then_inc(values0_swapped, 16)
                if real(i):
                    sp.wait_ge(srcdst_copied, i + 1)
                    sp.sem_inc(sp_passed, 1)
                    sp.dma_start(d_scratch[i].rearrange("g h m -> h g m"),
                                 sdT[0:HEADS0, :].rearrange("h (g m) -> h g m", m=N)).then_inc(dst_stored, 16)
                    sp.wait_ge(dst_stored, 16 * (i + 1))
                    sp.sem_inc(sp_passed, 1)
                    if real(i - 1):
                        sp.wait_ge(probs0_turned, 6 * i)
                        sp.sem_inc(sp_passed, 1)
                    else:
                        sp.wait_ge(w_low, 3 * C)
                    for g in range(2):
                        src = d_scratch[i].rearrange("(t g) h m -> g t (h m)", g=2)[g:g + 1]
                        sp.dma_start(z[64 * g:64 * g + 64], src.broadcast_to((64, TILES, HEADS0 * N))).then_inc(dst_spread, 16)
                if real(j):
                    sp.wait_ge(values1_made, (j + 1) * TILES)
                    sp.sem_inc(sp_passed, 1)
                    if real(j - 1):
                        sp.wait_ge(attn1_full, 2 * j)
                        sp.sem_inc(sp_passed, 1)
                    for g in range(2):
                        sp.dma_start(V1s[64 * g:64 * g + 64], V1[64 - 64 * g:128 - 64 * g]).then_inc(values1_swapped, 16)
                if real(j):
                    sp.wait_ge(out_made, (j + 1) * TILES)
                    sp.sem_inc(sp_passed, 1)
                    sp.dma_start(out_v[j], thT[:].rearrange("p c n -> p (c n)").rearrange("p (t d) -> p t d", d=D)).then_inc(out_stored, 16)

            iterations(sp, body)
            sp.wait_ge(out_stored, 16 * groups)

        @block.gpsimd
        def _(pool):
            pool.memset(ident[:], 0.0).then_inc(zeros_made, 1)
            pool.memset(ident_b[:], 0.0).then_inc(zeros_made, 1)
            pool.memset(wsd[:], 0.0).then_inc(consts_made, 1)
            pool.memset(hb_rows[:].bitcast(F32), 0.0).then_inc(consts_made, 1)
            pool.memset(V0[:, :, :, E0:E0 + 1], 1.0).then_inc(consts_made, 1)
            pool.memset(V1[:, :, :, E1:E1 + 1], 1.0).then_inc(consts_made, 1)
            pool.memset(masked0[:], MASKED0).then_inc(consts_made, 1)
            pool.memset(minus1[:], -1.0).then_inc(consts_made, 1)
            pool.memset(half[:], 0.5).then_inc(consts_made, 1)
            pool.memset(minus_half[:], -0.5).then_inc(consts_made, 1)
            pool.wait_ge(zeros_made, 2)
            for m in (ident, ident_b):
                pool.affine_select(out=m[:], in_=m[:], compare_op=ALU.not_equal, fill=1.0, base=0,
                                   pattern=[[-1, P]], channel_multiplier=1).then_inc(consts_made, 1)
            pool.wait_ge(consts_made, 10)

            def inv_std(layer, g):
                pool.wait_ge((moments0, moments1)[layer], TILES * (g + 1))
                pool.sem_inc(pool_passed, 1)
                pool.tensor_scalar(ve[:, layer], mv[:, layer, :, 1], EPS, None, ALU.add).then_inc((var0_eps, var1_eps)[layer], 1)
                pool.wait_ge((var0_eps, var1_eps)[layer], g + 1)
                if real(g - 1):
                    pool.wait_ge((xn0_made, xn1_made)[layer], TILES * g)
                pool.tensor_tensor(rstd[:, layer], ve[:, layer], minus_half[:], ALU.pow).then_inc((inv_std0, inv_std1)[layer], 1)

            inv_std(0, 0)

            def body(i, par):
                if not real(i):
                    return
                if real(i + 1):
                    inv_std(0, i + 1)
                pool.wait_ge(dst_spread, 32 * (i + 1))
                pool.wait_ge(src_copied, i + 1)
                for t in range(TILES):
                    zt = z[:, t].rearrange("p (h m) -> p h m", m=N)
                    pool.tensor_tensor(zt, zt, s_tok[:, t, HEADS0:].unsqueeze(2).broadcast_to((P, HEADS0, N)),
                                       ALU.add).then_inc(scores0_summed, 1)
                for t in range(TILES):
                    if real(i - 1):
                        pool.wait_ge(out_made, TILES * (i - 1) + t + 1)
                    pool.wait_ge(gated, TILES * i + t + 1)
                    pool.tensor_tensor(x2[:, t], x_in[:, par, t], ee[:, t], ALU.subtract).then_inc(x2_made, 1)
                inv_std(1, i)
                pool.wait_ge(xn1_made, TILES * (i + 1))
                for t in range(TILES):
                    pool.tensor_tensor(x2[:, t], x2[:, t], bf_row[:], ALU.add).then_inc(x2_biased, 1)

            iterations(pool, body)

        @block.scalar
        def _(act):
            def h0_parts(g):
                if real(g - 1):
                    act.wait_ge(gate_full, TILES * g)
                for c in range(C):
                    act.wait_ge(xn0_turned, C * g + c + 1)
                    act.activation(hT0h[:, c], ps[:, job("h0_low", c) % BANKS], ACT.Relu).then_inc(h0_high, 1)

            act.wait_ge(hw_turned, 3)
            for c in range(C):
                act.activation(wh["Hw"][:, c, :], ps[:, c, 0:D], ACT.Copy).then_inc(w_high, 1)
            act.wait_ge(w_loaded["W0"], 16 * C)
            for c in range(C):
                act.activation(wh["W0"][:, c, :], staged["W0"][:, c], ACT.Copy).then_inc(w0_high, 1)
            h0_parts(0)
            act.wait_ge(consts_loaded, 16 * 9)
            act.wait_ge(consts_made, 10)
            for r in (0, 32):
                act.activation(hb_rows[r:r + 1, :], x2[r:r + 1, 0, :], ACT.Copy).then_inc(rows_made, 1)
            act.activation(ones_rows[:], ident[0:33, :], ACT.Identity, scale=0.0, bias=1.0).then_inc(rows_made, 1)
            for name in w_late:
                act.wait_ge(w_loaded[name], 16)
                for c in range(C):
                    act.activation(wh[name][:, c, :], staged[name][:, c], ACT.Copy).then_inc(w_high, 1)

            def body(i, par):
                j = i - 1
                if real(i):
                    for t in range(TILES):
                        act.wait_ge(values0_made, TILES * i + t + 1)
                        if real(i - 1):
                            act.wait_ge(x2_made, TILES * (i - 1) + t + 1)
                        act.activation(ee[:, t], ps[:, job("th_made", t) % BANKS, 0:D], ACT.Tanh).then_inc(th_made, 1)
                        act.wait_ge(gate_full, TILES * i + t + 1)
                        if real(i - 1):
                            act.wait_ge(gated, TILES * (i - 1) + t + 1)
                        act.activation(gate[:, t], ps[:, job("gate_tanh", t) % BANKS, 0:D], ACT.Tanh, scale=0.5).then_inc(gate_tanh, 1)
                if real(j):
                    if real(j - 1):
                        act.wait_ge(final_full, TILES * j)
                    for c in range(C):
                        act.wait_ge(xn1_turned, C * j + c + 1)
                        act.activation(hT1h[:, c], ps[:, job("h1_low", c) % BANKS], ACT.Relu).then_inc(h1_high, 1)
                if real(i):
                    if real(i - 2):
                        act.wait_ge(out_stored, 16 * (i - 1))
                    for c in range(C):
                        act.wait_ge(th_turned, C * i + c + 1)
                        act.activation(thT[:, c], ps[:, job("thT_copied", c) % BANKS], ACT.Copy).then_inc(thT_copied, 1)

                def copy_biased(chunks, full, copied, name, bias, at):
                    for c in chunks:
                        act.wait_ge(full, C * j + c + 1)
                        act.activation(big[:, at + c], ps[:, job(name, c) % BANKS], ACT.Identity,
                                       bias=bias[:, c:c + 1]).then_inc(copied, 1)

                if real(j):
                    act.wait_ge(attn0_full, 2 * (j + 1))
                    copy_biased([0], q_full, q_copied, "q_copied", bq_col, 0)
                if real(i):
                    act.wait_ge(srcdst_full, i + 1)
                    if real(i - 1):
                        act.wait_ge(dst_stored, 16 * i)
                    act.activation(sdT[:], ps[0:2 * HEADS0, job("src_copied", 0) % BANKS], ACT.Copy).then_inc(srcdst_copied, 1)
                if real(j):
                    copy_biased([1, 2], q_full, q_copied, "q_copied", bq_col, 0)
                    copy_biased(range(C), k_full, k_copied, "k_copied", bk_col, 3)
                if real(i):
                    for t in range(TILES):
                        act.wait_ge(gate_tanh, TILES * i + t + 1)
                        act.activation(gate[:, t], gate[:, t], ACT.Identity, scale=0.5, bias=half[:]).then_inc(gate_made, 1)

                def exp0(t):
                    if real(i):
                        act.wait_ge(scores0_shifted, TILES * i + t + 1)
                        act.activation(z[:, t], z[:, t], ACT.Exp).then_inc(probs0_made, 1)

                def exp1(t):
                    if real(j):
                        act.wait_ge(scores1_shifted, 4 * j + 2 * (t // 2) + 2)
                        act.activation(p1[:, t], p1[:, t], ACT.Exp, scale=float(E1) ** -0.5).then_inc(probs1_made, 1)

                exp0(0)
                exp1(0)
                exp1(1)
                if real(i + 1):
                    h0_parts(i + 1)
                exp1(2)
                exp1(3)
                if real(j):
                    if real(i):
                        act.wait_ge(srcdst_full, i + 1)
                    else:
                        act.wait_ge(out_stored, 16 * j)
                    for c in range(3):
                        act.wait_ge(probs1_turned, 3 * j + c + 1)
                        act.activation(thT[:, c], ps[:, job("probs1T_copied", c) % BANKS], ACT.Copy).then_inc(probs1T_copied, 1)
                exp0(1)
                exp0(2)
                exp0(3)
                if real(i):
                    if real(i - 1):
                        act.wait_ge(scores1_full, 2 * i)
                    else:
                        act.wait_ge(w_low, C)
                    for q in range(6):
                        act.wait_ge(probs0_turned, 6 * i + q + 1)
                        act.activation(big[:, q], ps[:, job("probs0T_copied", q) % BANKS], ACT.Copy).then_inc(probs0T_copied, 1)
                if real(j):
                    act.wait_ge(values1_full, TILES * (j + 1))
                    for c in range(C):
                        act.wait_ge(attn1_turned, C * j + c + 1)
                        act.activation(hT1h[:, c], ps[:, job("attn1_low", c) % BANKS], ACT.Copy).then_inc(attn1_high, 1)
                if real(i):
                    for t in range(TILES):
                        act.wait_ge(attn0_made, 4 * i + 2 * (t // 2) + 2)
                        act.activation(ee[:, t], x1[:, t], ACT.Exp, bias=minus1[:]).then_inc(elu_exp, 1)

            iterations(act, body)

        @block.tensor
        def _(pe):
            def turn(dst, src, rows=P):
                return pe.transpose(dst, src, ident[0:rows, 0:rows])

            def take(i, at):
                reader = last_reader(i, at)
                if reader is not None:
                    pe.wait_ge(*reader)
                return ps[:, at % BANKS]

            def product(dst, left_h, left_l, right_h, right_l, more=False):
                for c in range(C):
                    pe.matmul(dst, left_h(c), right_h(c), start=(c == 0), stop=False)
                    pe.matmul(dst, left_h(c), right_l(c), start=False, stop=False)
                    mm = pe.matmul(dst, left_l(c), right_h(c), start=False, stop=(c == C - 1 and not more))
                return mm

            pe.wait_ge(consts_made, 10)
            pe.wait_ge(hw_loaded, 16)
            for c in range(C):
                for f in range(C):
                    mm = turn(ps[:, c, f * P:(f + 1) * P], staged["Hw"][:, f, c * P:(c + 1) * P])
                mm.then_inc(hw_turned, 1)

            def turn_tokens(name, done, src, i, g):
                for c in range(C):
                    take(i, job(name, c))
                    for t in range(TILES):
                        mm = turn(ps[:, job(name, c) % BANKS, t * P:(t + 1) * P], src(t, c))
                    mm.then_inc(done, 1)

            def turn_h0(it, g, par):
                pe.wait_ge(xn0_made, TILES * (g + 1))
                turn_tokens("h0_low", xn0_turned, lambda t, c: xn0[:, par, t, c * P:(c + 1) * P], it, g)

            turn_h0(NEXT, 0, 0)
            pe.wait_ge(small_ready, 5)
            pe.wait_ge(rows_made, 3)
            pe.wait_ge(w0_low, C)

            def body(i, par):
                j = i - 1
                if real(i):
                    pe.wait_ge(h0_low, C * (i + 1))
                    for t in range(TILES):
                        toks = slice(t * P, (t + 1) * P)
                        take(i, job("th_made", t))
                        product(ps[:, job("th_made", t) % BANKS, 0:D], lambda c: hT0h[:, c, toks], lambda c: hT0l[:, c, toks],
                                lambda c: wh["W0"][:, c], lambda c: wl["W0"][:, c]).then_inc(values0_full, 1)
                        take(i, job("gate_tanh", t))
                        dst = ps[:, job("gate_tanh", t) % BANKS, 0:D]
                        product(dst, lambda c: hT0h[:, c, toks], lambda c: hT0l[:, c, toks],
                                lambda c: wh["Hw"][:, c], lambda c: wl["Hw"][:, c], more=True)
                        pe.matmul(dst, ones_rows[:], hb_rows[:], start=False, stop=True).then_inc(gate_full, 1)
                if real(j):
                    pe.wait_ge(xn1_made, TILES * (j + 1))
                    turn_tokens("h1_low", xn1_turned, lambda t, c: p1[:, t, c * P:(c + 1) * P], i, j)
                if real(i):
                    pe.wait_ge(th_made, TILES * (i + 1))
                    turn_tokens("thT_copied", th_turned, lambda t, c: ee[:, t, c * P:(c + 1) * P], i, i)

                def project(o, full, name, w):
                    take(i, job(name, o))
                    cols = slice(o * P, (o + 1) * P)
                    product(ps[:, job(name, o) % BANKS], lambda c: wh[w][:, c, cols], lambda c: wl[w][:, c, cols],
                            lambda c: hT1h[:, c], lambda c: hT1l[:, c]).then_inc(full, 1)

                if real(j):
                    if not real(j - 1):
                        pe.wait_ge(w_low, C * 4)
                    pe.wait_ge(h1_low, C * (j + 1))
                    project(0, q_full, "q_copied", "Wq")
                if real(i):
                    pe.wait_ge(thT_copied, C * (i + 1))
                    take(i, job("src_copied", 0))
                    for c in range(C):
                        mm = pe.matmul(ps[0:2 * HEADS0, job("src_copied", 0) % BANKS], wsd[:, c], thT[:, c],
                                       start=(c == 0), stop=(c == C - 1))
                    mm.then_inc(srcdst_full, 1)
                if real(j):
                    project(1, q_full, "q_copied", "Wq")
                    project(2, q_full, "q_copied", "Wq")
                if real(i):
                    pe.wait_ge(srcdst_copied, i + 1)
                    pe.sem_inc(pe_passed, 1)
                    for t in range(TILES):
                        mm = turn(ps[:, job("src_copied", 0) % BANKS, t * 2 * HEADS0:(t + 1) * 2 * HEADS0],
                                  sdT[:, t * P:(t + 1) * P], 2 * HEADS0)
                    mm.then_inc(srcdst_turned, 1)
                if real(j):
                    project(0, k_full, "k_copied", "Wk")
                    project(1, k_full, "k_copied", "Wk")
                    project(2, k_full, "k_copied", "Wk")
                    for t in range(TILES):
                        toks = slice(t * P, (t + 1) * P)
                        take(i, job("values1_made", t))
                        product(ps[:, job("values1_made", t) % BANKS, 0:D], lambda c: hT1h[:, c, toks], lambda c: hT1l[:, c, toks],
                                lambda c: wh["Wv"][:, c], lambda c: wl["Wv"][:, c]).then_inc(values1_full, 1)

                def scores(pair):
                    tiles = slice(2 * pair, 2 * pair + 2)
                    banks = []
                    for odd in range(2):
                        take(i, job("scores1_shifted", 2 * pair + odd))
                        bank = ps[:, job("scores1_shifted", 2 * pair + odd) % BANKS, 0:D].rearrange("p (t h m) -> p t h m", t=2, m=N)
                        pe.matmul(bank, ident_b[:], mask1[:, tiles].unsqueeze(2).broadcast_to((P, 2, PAIRS1, N)),
                                  start=True, stop=False, skip_group_check=True)
                        banks.append(bank)
                    for t in range(2):
                        for h in range(HEADS1):
                            r = 64 * (h % 2)
                            for g in range(2):
                                at = (2 * pair + t) * P + g * N
                                mm = pe.matmul(banks[h % 2][g * N:(g + 1) * N, t, h // 2], big[r:r + E1, h // 2, at:at + N],
                                               big[r:r + E1, 3 + h // 2, at:at + N], start=False, stop=True,
                                               skip_group_check=True)
                    mm.then_inc(scores1_full, 1)

                if real(j):
                    pe.wait_ge(q_copied, C * (j + 1))
                    pe.wait_ge(k_copied, C * (j + 1))
                    pe.wait_ge(mask1_made, j + 1)
                    scores(0)
                    scores(1)
                if real(i + 1):
                    turn_h0(i, i + 1, 1 - par)

                def turn_probs(name, ready, done, src, pairs, g, jobs):
                    for q in range(jobs):
                        take(i, job(name, q))
                        for k in range(4):
                            t, pair = divmod(4 * q + k, pairs)
                            if k == 0 or pair == 0:
                                pe.wait_ge(ready, TILES * g + t + 1)
                            mm = turn(ps[:, job(name, q) % BANKS, k * P:(k + 1) * P], src[:, t, pair * P:(pair + 1) * P])
                        mm.then_inc(done, 1)

                def attend(pair, name, done, ready, swapped, probsT, V, Vs, heads, width, g_, ready_n):
                    pairs = heads // 2
                    last = ((2 * pair + 2) * pairs - 1) // 4
                    pe.wait_ge(swapped, 32 * (g_ + 1))
                    pe.sem_inc(pe_passed, 1)
                    pe.wait_ge(ready, ready_n * g_ + last + 1)
                    pe.sem_inc(pe_passed, 1)
                    for odd in range(2):
                        take(i, job(name, 2 * pair + odd))
                        pe.sem_inc(pe_passed, 1)
                    banks = [ps[:, job(name, 2 * pair + odd) % BANKS, 0:heads * (width + 1)]
                             .rearrange("p (t h e) -> p t h e", t=2, e=width + 1) for odd in range(2)]
                    for t in range(2 * pair, 2 * pair + 2):
                        for h in range(heads):
                            q, k = divmod(t * pairs + h // 2, 4)
                            r = 64 * (h % 2)
                            for g in range(2):
                                vals = V if h % 2 == g else Vs
                                mm = pe.matmul(banks[h % 2][g * N:(g + 1) * N, t % 2, h // 2],
                                               probsT[r:r + N, q, k * P + g * N:k * P + (g + 1) * N],
                                               vals[r:r + N, t, h], start=True, stop=True, skip_group_check=True)
                    mm.then_inc(done, 1)

                def attend1(pair):
                    attend(pair, "attn1_made", attn1_full, probs1T_copied, values1_swapped, thT, V1, V1s, HEADS1, E1, j, 3)

                def attend0(pair):
                    attend(pair, "attn0_made", attn0_full, probs0T_copied, values0_swapped, big, V0, V0s, HEADS0, E0, i, 6)

                if real(j):
                    turn_probs("probs1T_copied", probs1_made, probs1_turned, p1, PAIRS1, j, 3)
                    attend1(0)
                    attend1(1)
                if real(i):
                    turn_probs("probs0T_copied", probs0_made, probs0_turned, z, PAIRS0, i, 6)
                    attend0(0)
                if real(j):
                    pe.wait_ge(attn1_made, TILES * (j + 1))
                    turn_tokens("attn1_low", attn1_turned, lambda t, c: p1[:, t, c * P:(c + 1) * P], i, j)
                if real(i):
                    attend0(1)
                if real(j):
                    pe.wait_ge(attn1_low, C * (j + 1))
                    for t in range(TILES):
                        toks = slice(t * P, (t + 1) * P)
                        take(i, job("out_made", t))
                        product(ps[:, job("out_made", t) % BANKS, 0:D], lambda c: hT1h[:, c, toks], lambda c: hT1l[:, c, toks],
                                lambda c: wh["Wf"][:, c], lambda c: wl["Wf"][:, c]).then_inc(final_full, 1)

            iterations(pe, body)

        @block.vector
        def _(dve):
            def row_stats(layer, src, t, g):
                dve.bn_stats(stats[:, layer, t], src).then_inc((stats0, stats1)[layer], 1)

            def row_sums(layer, g):
                for t in range(TILES):
                    dve.wait_ge((stats0, stats1)[layer], TILES * g + t + 1)
                    dve.sem_inc(dve_passed, 1)
                    dve.bn_aggr(mv[:, layer, t], stats[:, layer, t]).then_inc((moments0, moments1)[layer], 1)

            def normalise(layer, src, dst, done, g):
                dve.wait_ge((inv_std0, inv_std1)[layer], g + 1)
                for t in range(TILES):
                    dve.tensor_scalar(dst(t), src(t), mv[:, layer, t, 0:1], rstd[:, layer, t:t + 1],
                                      ALU.subtract, ALU.mult).then_inc(done, 1)

            def norm0(g, par):
                dve.wait_ge(x_loaded[par], 8 * (g - par) + 16)
                for t in range(TILES):
                    row_stats(0, x_in[:, par, t], t, g)
                row_sums(0, g)

            def norm0_end(g, par):
                normalise(0, lambda t: x_in[:, par, t], lambda t: xn0[:, par, t], xn0_made, g)

            def h0_lows(g):
                for c in range(C):
                    dve.wait_ge(h0_high, C * g + c + 1)
                    dve.scalar_tensor_tensor(hT0l[:, c], ps[:, job("h0_low", c) % BANKS], 0.0, hT0h[:, c].bitcast(F32),
                                             ALU.max, ALU.subtract).then_inc(h0_low, 1)

            norm0(0, 0)
            norm0_end(0, 0)
            for c in range(C):
                dve.wait_ge(w_high, c + 1)
                dve.tensor_tensor(wl["Hw"][:, c, :], ps[:, c, 0:D], wh["Hw"][:, c, :].bitcast(F32), ALU.subtract)\
                    .then_inc(small_ready, 1)
            for c in range(C):
                dve.wait_ge(w0_high, c + 1)
                dve.tensor_tensor(wl["W0"][:, c, :], staged["W0"][:, c], wh["W0"][:, c, :].bitcast(F32),
                                  ALU.subtract).then_inc(w0_low, 1)
            h0_lows(0)
            dve.wait_ge(consts_loaded, 16 * 9)
            dve.wait_ge(consts_made, 10)
            dve.wait_ge(rows_made, 2)
            dve.tensor_tensor(hb_rows[32:33, :], x2[32:33, 0, :], hb_rows[32:33, :].bitcast(F32), ALU.subtract)\
                .then_inc(small_ready, 1)
            for k, col in ((0, wcol), (HEADS0, wcol2)):
                for q in range(4):
                    rows = slice(32 * q, 32 * q + 32)
                    for c in range(C):
                        at = k + 4 * c + q
                        dve.tensor_copy(wsd[rows, c, at:at + 1], col[rows, c:c + 1])
            dve.tensor_scalar(b0_plus1[:], b0_plus1[:], 1.0, None, ALU.add).then_inc(small_ready, 1)
            for n, name in enumerate(w_late):
                for c in range(C):
                    dve.wait_ge(w_high, C * (n + 1) + c + 1)
                    dve.tensor_tensor(wl[name][:, c, :], staged[name][:, c], wh[name][:, c, :].bitcast(F32),
                                      ALU.subtract).then_inc(w_low, 1)
            dve.wait_ge(small_ready, 5)

            def body(i, par):
                j = i - 1
                if real(i):
                    if real(i - 1):
                        dve.wait_ge(values0_swapped, 32 * i)
                    for t in range(TILES):
                        dve.wait_ge(values0_full, TILES * i + t + 1)
                        dve.tensor_tensor(V0[:, t, :, 0:E0], ps[:, job("th_made", t) % BANKS, 0:D].rearrange("p (h e) -> p h e", e=E0),
                                          b0_plus1[:].unsqueeze(1).broadcast_to((P, HEADS0, E0)), ALU.add)\
                            .then_inc(values0_made, 1)
                    dve.wait_ge(adj_loaded[par], 8 * (i - par) + 16)
                    if real(i - 1):
                        dve.wait_ge(masked, TILES * i)
                    dve.tensor_scalar(not_adj[:], adj_in[:, par], 0.0, None, ALU.is_equal).then_inc(not_adj_made, 1)
                if real(j):
                    for c in range(C):
                        dve.wait_ge(h1_high, C * j + c + 1)
                        dve.scalar_tensor_tensor(hT1l[:, c], ps[:, job("h1_low", c) % BANKS], 0.0, hT1h[:, c].bitcast(F32),
                                                 ALU.max, ALU.subtract).then_inc(h1_low, 1)
                if real(i + 1):
                    norm0(i + 1, 1 - par)
                    norm0_end(i + 1, 1 - par)
                if real(i):
                    dve.wait_ge(srcdst_turned, i + 1)
                    if real(i - 1):
                        dve.wait_ge(scores0_summed, TILES * i)
                    dve.tensor_copy(s_tok[:].rearrange("p t h -> p (t h)"),
                                    ps[:, job("src_copied", 0) % BANKS, 0:TILES * 2 * HEADS0]).then_inc(src_copied, 1)

                def values1(t):
                    if real(j):
                        dve.wait_ge(values1_full, TILES * j + t + 1)
                        dve.tensor_tensor(V1[:, t, :, 0:E1], ps[:, job("values1_made", t) % BANKS, 0:D].rearrange("p (h e) -> p h e", e=E1),
                                          bv_row[:].rearrange("p (h e) -> p h e", e=E1), ALU.add).then_inc(values1_made, 1)

                def shift1(pair):
                    tiles = slice(2 * pair, 2 * pair + 2)
                    dve.wait_ge(scores1_full, 2 * j + pair + 1)
                    for odd in range(2):
                        n = 4 * j + 2 * pair + odd + 1
                        bank = ps[:, job("scores1_shifted", 2 * pair + odd) % BANKS, 0:D].rearrange("p (t h m) -> p t h m", t=2, m=N)
                        top = mx1[:, tiles].rearrange("p t (h o) -> p t h o", o=2)[:, :, :, odd]
                        dve.tensor_reduce(top, bank, AX_X, ALU.max).then_inc(max1_made, 1)
                        dve.wait_ge(max1_made, n)
                        dve.tensor_tensor(p1[:, tiles].rearrange("p t (h o m) -> p t h o m", o=2, m=N)[:, :, :, odd], bank,
                                          top.unsqueeze(3).broadcast_to((P, 2, PAIRS1, N)), ALU.subtract)\
                            .then_inc(scores1_shifted, 1)

                def softmax0(t):
                    n = TILES * i + t + 1
                    zt = z[:, t].rearrange("p (h m) -> p h m", m=N)
                    dve.wait_ge(scores0_summed, n)
                    dve.scalar_tensor_tensor(z[:, t], z[:, t], SLOPE, z[:, t], ALU.mult, ALU.max).then_inc(leaky_made, 1)
                    dve.wait_ge(leaky_made, n)
                    dve.sem_inc(dve_passed, 1)
                    dve.wait_ge(not_adj_made, i + 1)
                    dve.sem_inc(dve_passed, 1)
                    dve.copy_predicated(zt, not_adj[:, t].unsqueeze(1).broadcast_to((P, HEADS0, N)),
                                        masked0[:].unsqueeze(2).broadcast_to((P, HEADS0, N))).then_inc(masked, 1)
                    dve.wait_ge(masked, n)
                    dve.tensor_reduce(mx0[:, t], zt, AX_X, ALU.max).then_inc(max0_made, 1)
                    dve.wait_ge(max0_made, n)
                    dve.tensor_tensor(zt, zt, mx0[:, t].unsqueeze(2).broadcast_to((P, HEADS0, N)), ALU.subtract)\
                        .then_inc(scores0_shifted, 1)

                def divide(u, name, full, dst, sums, inverted, done, heads, width, g):
                    pair, odd = divmod(u, 2)
                    tiles = slice(2 * pair, 2 * pair + 2)
                    v = ps[:, job(name, u) % BANKS, 0:heads * (width + 1)].rearrange("p (t h e) -> p t h e", t=2, e=width + 1)
                    inv = sums[:, tiles].rearrange("p t (h o) -> p t h o", o=2)[:, :, :, odd]
                    dve.wait_ge(full, 2 * g + pair + 1)
                    dve.reciprocal(inv, v[:, :, :, width]).then_inc(inverted, 1)
                    dve.wait_ge(inverted, 4 * g + u + 1)
                    dve.tensor_tensor(dst[:, tiles].rearrange("p t (h o e) -> p t h o e", o=2, e=width)[:, :, :, odd],
                                      v[:, :, :, 0:width], inv.unsqueeze(3).broadcast_to((P, 2, heads // 2, width)),
                                      ALU.mult).then_inc(done, 1)

                def close(t):
                    n = TILES * i + t + 1
                    dve.wait_ge(elu_exp, n)
                    dve.scalar_tensor_tensor(ee[:, t], ee[:, t], 1.0, x1[:, t], ALU.min, ALU.max).then_inc(elu_made, 1)
                    dve.scalar_tensor_tensor(x_in[:, par, t], xn0[:, par, t], 0.0, x_in[:, par, t], ALU.max, ALU.add)\
                        .then_inc(x_plus_h, 1)
                    dve.wait_ge(elu_made, n)
                    dve.scalar_tensor_tensor(x1[:, t], xn0[:, par, t], 0.0, ee[:, t], ALU.max, ALU.subtract)\
                        .then_inc(h_less_elu, 1)
                    dve.wait_ge(h_less_elu, n)
                    dve.wait_ge(x_plus_h, n)
                    dve.wait_ge(gate_made, n)
                    dve.scalar_tensor_tensor(ee[:, t], x1[:, t], 1.0, gate[:, t], ALU.add, ALU.mult).then_inc(gated, 1)

                def divide0(pair):
                    for odd in range(2):
                        divide(2 * pair + odd, "attn0_made", attn0_full, x1, rs0, inv0_made, attn0_made, HEADS0, E0, i)

                def add_out(t):
                    if real(j):
                        dve.wait_ge(final_full, TILES * j + t + 1)
                        dve.tensor_tensor(thT[:].rearrange("p c n -> p (c n)")[:, t * D:(t + 1) * D],
                                          ps[:, job("out_made", t) % BANKS, 0:D], x2[:, t], ALU.add).then_inc(out_made, 1)

                def divide1(pair):
                    for u in (2 * pair, 2 * pair + 1):
                        divide(u, "attn1_made", attn1_full, p1, rs1, inv1_made, attn1_made, HEADS1, E1, j)

                if real(j):
                    if real(j - 1):
                        dve.wait_ge(values1_swapped, 32 * j)
                    for t in range(TILES):
                        values1(t)
                if real(i):
                    softmax0(0)
                if real(j):
                    shift1(0)
                    shift1(1)
                if real(i + 1):
                    h0_lows(i + 1)
                if real(i):
                    if real(j):
                        dve.wait_ge(scores1_full, 2 * (j + 1))
                    dve.tensor_scalar(mask1[:], adj_in[:, par], -1.0, MASKED1 * float(E1) ** 0.5, ALU.add, ALU.mult)\
                        .then_inc(mask1_made, 1)
                    softmax0(1)
                    softmax0(2)
                if real(j):
                    dve.wait_ge(probs1_turned, 3 * (j + 1))
                    divide1(0)
                if real(i):
                    softmax0(3)
                if real(j):
                    divide1(1)
                if real(i):
                    divide0(0)
                if real(j):
                    for c in range(C):
                        dve.wait_ge(attn1_high, C * j + c + 1)
                        dve.tensor_tensor(hT1l[:, c], ps[:, job("attn1_low", c) % BANKS], hT1h[:, c].bitcast(F32), ALU.subtract)\
                            .then_inc(attn1_low, 1)
                    dve.wait_ge(x2_biased, TILES * (j + 1))
                if real(i):
                    close(0)
                    close(1)
                    divide0(1)
                add_out(0)
                add_out(1)
                if real(i):
                    close(2)
                add_out(2)
                if real(i):
                    close(3)
                add_out(3)
                if real(i):
                    for t in range(TILES):
                        dve.wait_ge(x2_made, TILES * i + t + 1)
                        row_stats(1, x2[:, t], t, i)
                    row_sums(1, i)
                    if real(j):
                        dve.wait_ge(attn1_turned, C * (j + 1))
                    normalise(1, lambda t: x2[:, t], lambda t: p1[:, t], xn1_made, i)

            iterations(dve, body)


_INS = ['x', 'adj', 'L0_gnn_W', 'L0_gnn_b', 'L0_gnn_w_src', 'L0_gnn_w_dst', 'L0_gnn_H_w', 'L0_gnn_H_b', 'L1_gnn_Wq',
        'L1_gnn_bq', 'L1_gnn_Wk', 'L1_gnn_bk', 'L1_gnn_Wv', 'L1_gnn_bv', 'L1_gnn_Wf', 'L1_gnn_bf']


def kernel(**inputs):
    import concourse.bacc as _bacc
    from concourse.bass_utils import run_bass_kernel_spmd as _run

    nc = _bacc.Bacc("TRN2", target_bir_lowering=False, num_devices=1)
    arrays, args = {}, []
    for name in _INS:
        a = np.ascontiguousarray(inputs[name])
        arrays[f"in_{name}_dram"] = a
        args.append(nc.dram_tensor(f"in_{name}_dram", a.shape, mybir.dt.from_np(a.dtype), kind="ExternalInput").ap())
    shape = np.shape(inputs['x'])
    graphs = 2 * TILES
    out = nc.dram_tensor("out_0_dram", shape, F32, kind="ExternalOutput").ap()
    scratch = nc.dram_tensor("d_scratch", (shape[0] // graphs, graphs, HEADS0, N), F32, kind="Internal").ap()
    two_layer_gnn(nc, *args, out, scratch)
    r = _run(nc, [arrays], core_ids=[0])
    return r.results[0]["out_0_dram"]
```

```python
from contextlib import ExitStack

import numpy as np

import concourse.bass as bass
from concourse import mybir

ACT = mybir.ActivationFunctionType
ALU = mybir.AluOpType
AX_X = mybir.AxisListType.X
F32 = mybir.dt.float32
F32R = mybir.dt.float32r
BF16 = mybir.dt.bfloat16
U8 = mybir.dt.uint8

P = 128
N = 64
D = 384
C = D // P
TILES = 4
TOK = TILES * P
HEADS0, E0 = 12, 32
HEADS1, E1 = 6, 64
PAIRS0, PAIRS1 = HEADS0 // 2, HEADS1 // 2
BANKS = 8
SLOPE = 0.2
MASKED0 = -999.0
MASKED1 = 9e15
EPS = 1e-5

def two_layer_gnn(nc, x, adj, W0, b0, w_src, w_dst, H_w, H_b, Wq, bq, Wk, bk, Wv, bv, Wf, bf, out, d_scratch):
    groups = x.shape[0] * x.shape[1] // TOK
    x_v = x.rearrange("a n d -> (a n) d").rearrange("(i t p) d -> i p t d", t=TILES, p=P)
    out_v = out.rearrange("a n d -> (a n) d").rearrange("(i t p) d -> i p t d", t=TILES, p=P)
    adj_v = adj.rearrange("a n m -> (a n) m").rearrange("(i t p) m -> i p t m", t=TILES, p=P)

    with ExitStack() as ctx:
        def sb(name, shape, dt=F32):
            return ctx.enter_context(nc.sbuf_tensor(name, shape, dt))

        def sem(name):
            return ctx.enter_context(nc.semaphore(name))

        wh = {k: sb(f"{k}_hi", [P, C, D], F32R) for k in ("W0", "Hw", "Wq", "Wk", "Wv", "Wf")}
        wl = {k: sb(f"{k}_lo", [P, C, D], F32R) for k in ("W0", "Hw", "Wq", "Wk", "Wv", "Wf")}
        wsd = sb("wsd", [P, C, 2 * HEADS0])
        hb_rows = sb("hb_rows", [33, D], F32R)
        ones_rows = sb("ones_rows", [33, P], F32R)
        b0_plus1 = sb("b0_plus1", [P, E0])
        bq_col = sb("bq_col", [P, C])
        bk_col = sb("bk_col", [P, C])
        bv_row = sb("bv_row", [P, D])
        bf_row = sb("bf_row", [P, D])
        ident = sb("ident", [P, P])
        ident_b = sb("ident_b", [P, P], BF16)
        masked0 = sb("masked0", [P, 1])
        minus1 = sb("minus1", [P, 1])
        half = sb("half", [P, 1])
        minus_half = sb("minus_half", [P, TILES])

        x_in = sb("x_in", [P, 2, TILES, D])
        xn0 = sb("xn0", [P, 2, TILES, D])
        adj_in = sb("adj_in", [P, 2, TILES, N], U8)
        hT0h = sb("hT0h", [P, C, TOK], F32R)
        hT0l = sb("hT0l", [P, C, TOK], F32R)
        hT1h = sb("hT1h", [P, C, TOK], F32R)
        hT1l = sb("hT1l", [P, C, TOK], F32R)
        gate = sb("gate", [P, TILES, D])
        V0 = sb("V0", [P, 2, TILES, 2, E0 + 1, PAIRS0])
        thT = sb("thT", [P, C, TOK])
        sdT = sb("sdT", [2 * HEADS0, TOK])
        s_tok = sb("s_tok", [P, TILES, 2 * HEADS0])
        z = sb("z", [P, TILES, HEADS0 * N])
        QT = sb("QT", [P, C, TOK])
        K_blocks = sb("K_blocks", [P, PAIRS1, TOK // N, 2, N])
        x1 = sb("x1", [P, TILES, D])
        ee = sb("ee", [P, TILES, D])
        x2 = sb("x2", [P, TILES, D])
        V1 = sb("V1", [P, 2, TILES, 2, E1 + 1, PAIRS1])
        p1 = sb("p1", [P, TILES, D])
        not_adj = sb("not_adj", [P, TILES, N], U8)
        mask1 = sb("mask1", [P, TILES, N], BF16)
        mx0 = sb("mx0", [P, TILES, HEADS0])
        rs0 = sb("rs0", [P, TILES, HEADS0])
        mx1 = sb("mx1", [P, TILES, HEADS1])
        rs1 = sb("rs1", [P, TILES, HEADS1])
        stats = sb("stats", [P, 2, TILES, 6])
        mv = sb("mv", [P, 2, TILES, 2])
        ve = sb("ve", [P, 2, TILES])
        rstd = sb("rstd", [P, 2, TILES])
        ps = ctx.enter_context(nc.psum_tensor("ps", [P, BANKS, 512], F32))
        staged = {"Hw": x1[:, 0:3], "W0": QT[:, :, 0:D], "Wq": thT[:, :, 0:D], 
                  "Wk": z[:, 0:2].rearrange("p t m -> p (t m)")[:, 0:C * D].rearrange("p (c d) -> p c d", d=D),
                  "Wv": z[:, 2:4].rearrange("p t m -> p (t m)")[:, 0:C * D].rearrange("p (c d) -> p c d", d=D),
                  "Wf": p1[:, 0:3]}

        hw_loaded = sem("hw_loaded")
        consts_loaded = sem("consts_loaded")
        consts_made = sem("consts_made")
        small_ready = sem("small_ready")
        w_high = sem("w_high")
        w_low = sem("w_low")
        hw_turned = sem("hw_turned")
        zeros_made = sem("zeros_made")
        ones_made = sem("ones_made")
        k_zeros_made = sem("k_zeros_made")
        rows_made = sem("rows_made")
        w_loaded = {k: sem(f"{k}_loaded") for k in ("W0", "Wq", "Wk", "Wv", "Wf")}
        w0_high = sem("w0_high")
        w0_low = sem("w0_low")
        x_loaded = [sem("x_loaded_0"), sem("x_loaded_1")]
        values0_spread = sem("values0_spread")
        values1_spread = sem("values1_spread")
        dst_stored = sem("dst_stored")
        dst_spread = sem("dst_spread")
        out_stored = sem("out_stored")
        adj_loaded = [sem("adj_loaded_0"), sem("adj_loaded_1")]
        xn0_turned = sem("xn0_turned")
        values0_full = sem("values0_full")
        gate_full = sem("gate_full")
        xn1_turned = sem("xn1_turned")
        q_full = sem("q_full")
        k_full = sem("k_full")
        values1_full = sem("values1_full")
        th_turned = sem("th_turned")
        srcdst_full = sem("srcdst_full")
        srcdst_turned = sem("srcdst_turned")
        scores1_full = sem("scores1_full")
        probs1_turned = sem("probs1_turned")
        attn1_full = sem("attn1_full")
        attn1_turned = sem("attn1_turned")
        final_full = sem("final_full")
        probs0_turned = sem("probs0_turned")
        attn0_full = sem("attn0_full")
        h0_high = sem("h0_high")
        th_made = sem("th_made")
        gate_tanh = sem("gate_tanh")
        gate_made = sem("gate_made")
        h1_high = sem("h1_high")
        q_copied = sem("q_copied")
        k_copied = sem("k_copied")
        thT_copied = sem("thT_copied")
        srcdst_copied = sem("srcdst_copied")
        probs1_made = sem("probs1_made")
        probs1T_copied = sem("probs1T_copied")
        attn1_high = sem("attn1_high")
        probs0_made = sem("probs0_made")
        probs0T_copied = sem("probs0T_copied")
        elu_exp = sem("elu_exp")
        stats0 = sem("stats0")
        moments0 = sem("moments0")
        xn0_made = sem("xn0_made")
        h0_low = sem("h0_low")
        values0_made = sem("values0_made")
        h1_low = sem("h1_low")
        values1_made = sem("values1_made")
        src_copied = sem("src_copied")
        max1_made = sem("max1_made")
        scores1_shifted = sem("scores1_shifted")
        not_adj_made = sem("not_adj_made")
        mask1_made = sem("mask1_made")
        leaky_made = sem("leaky_made")
        masked = sem("masked")
        max0_made = sem("max0_made")
        scores0_shifted = sem("scores0_shifted")
        inv1_made = sem("inv1_made")
        attn1_made = sem("attn1_made")
        attn1_low = sem("attn1_low")
        out_made = sem("out_made")
        inv0_made = sem("inv0_made")
        attn0_made = sem("attn0_made")
        elu_made = sem("elu_made")
        h_less_elu = sem("h_less_elu")
        x_plus_h = sem("x_plus_h")
        gated = sem("gated")
        stats1 = sem("stats1")
        moments1 = sem("moments1")
        xn1_made = sem("xn1_made")
        scores0_summed = sem("scores0_summed")
        var0_eps = sem("var0_eps")
        inv_std0 = sem("inv_std0")
        x2_made = sem("x2_made")
        var1_eps = sem("var1_eps")
        inv_std1 = sem("inv_std1")
        x2_biased = sem("x2_biased")
        sp_passed = sem("sp_passed")
        pool_passed = sem("pool_passed")
        pe_passed = sem("pe_passed")
        dve_passed = sem("dve_passed")

        def real(g):
            return not isinstance(g, int) or 0 <= g < groups

        def jobs(name, layer, signal, n):
            return [(name, layer, signal, n, k) for k in range(n)]

        pairs_of_jobs = zip(jobs("th_made", 0, th_made, 4), jobs("gate_tanh", 0, gate_tanh, 4))
        NEXT = -1
        RING = (
            [x for pair in pairs_of_jobs for x in pair]
            + jobs("h1_low", 1, h1_low, 3)
            + jobs("thT_copied", 0, thT_copied, 3)
            + jobs("q_copied", 1, q_copied, 3)[0:1]
            + jobs("src_copied", 0, src_copied, 1)
            + jobs("q_copied", 1, q_copied, 3)[1:3]
            + jobs("values1_made", 1, values1_made, 4)
            + jobs("h0_low", NEXT, h0_low, 3)
            + [("k_copied", 1, k_copied, 2 * C, 2 * c + 1) for c in range(C)]
            + jobs("scores1_shifted", 1, scores1_shifted, 4)
            + jobs("probs1T_copied", 1, probs1T_copied, 3)
            + jobs("attn1_made", 1, attn1_made, 4)
            + jobs("probs0T_copied", 0, probs0T_copied, 6)
            + jobs("attn0_made", 0, attn0_made, 4)[0:2]
            + jobs("attn1_low", 1, attn1_low, 3)
            + jobs("out_made", 1, out_made, 4)
            + jobs("attn0_made", 0, attn0_made, 4)[2:4]
        )
        assert len(RING) % BANKS == 0
        place = {(name, k): at for at, (name, _, _, _, k) in enumerate(RING)}

        def job(name, k):
            return place[name, 2 * k + 1 if name == "k_copied" else k]

        def last_reader(i, at):
            it = i
            while True:
                at -= BANKS
                if at < 0:
                    it, at = it - 1, at + len(RING)
                if isinstance(it, int) and it < NEXT:
                    return None
                _, layer, signal, n, k = RING[at]
                if real(it - layer):
                    return signal, (it - layer) * n + (k + 1)

        def iterations(eng, body):
            body(0, 0)
            body(1, 1)
            with eng.Fori(2, groups - 2, 2) as i:
                body(i, 0)
                body(i + 1, 1)
            body(groups - 2, 0)
            body(groups - 1, 1)
            body(groups, 0)

        w_late = ["Wq", "Wk", "Wv", "Wf"]
        w_source = {"Wq": Wq, "Wk": Wk, "Wv": Wv, "Wf": Wf}

        wcol, wcol2 = stats[:, 1, 0, 0:C], stats[:, 1, 1, 0:C]

        block = ctx.enter_context(nc.Block())

        @block.sync
        def _(sp):
            def load_x(i, par):
                if real(i - 2):
                    sp.wait_ge(x2_made, (i - 1) * TILES)
                    sp.sem_inc(sp_passed, 1)
                sp.dma_start(x_in[:, par], x_v[i]).then_inc(x_loaded[par], 16)
                if real(i - 2):
                    sp.wait_ge(mask1_made, i - 1)
                    sp.sem_inc(sp_passed, 1)
                sp.dma_start(adj_in[:, par], adj_v[i]).then_inc(adj_loaded[par], 16)

            sp.dma_start(x_in[:, 0], x_v[0]).then_inc(x_loaded[0], 16)
            sp.dma_start(staged["Hw"], H_w.rearrange("(c p) n -> p c n", p=P)).then_inc(hw_loaded, 16)
            for c in range(C):
                sp.dma_start(staged["W0"][:, c, :].rearrange("p (a e) -> p a e", e=E0),
                             W0[:, c * P:(c + 1) * P, :].rearrange("a p e -> p a e")).then_inc(w_loaded["W0"], 16)
            sp.dma_start(b0_plus1[:], b0.rearrange("(a e) -> a e", a=1).broadcast_to((P, E0))).then_inc(consts_loaded, 16)
            sp.dma_start(x2[0:1, 0, :], H_b.rearrange("(a e) -> a e", a=1)).then_inc(consts_loaded, 16)
            sp.dma_start(x2[32:33, 0, :], H_b.rearrange("(a e) -> a e", a=1)).then_inc(consts_loaded, 16)
            sp.dma_start(wcol, w_dst.rearrange("a e o -> (a e o)").rearrange("(c p) -> p c", p=P), allow_slow_non_contiguous=True).then_inc(consts_loaded, 16)
            sp.dma_start(wcol2, w_src.rearrange("a e o -> (a e o)").rearrange("(c p) -> p c", p=P), allow_slow_non_contiguous=True).then_inc(consts_loaded, 16)
            sp.dma_start(bq_col[:], bq.rearrange("(c p) -> p c", p=P), allow_slow_non_contiguous=True).then_inc(consts_loaded, 16)
            sp.dma_start(bk_col[:], bk.rearrange("(c p) -> p c", p=P), allow_slow_non_contiguous=True).then_inc(consts_loaded, 16)
            sp.dma_start(bv_row[:], bv.rearrange("(a e) -> a e", a=1).broadcast_to((P, D))).then_inc(consts_loaded, 16)
            sp.dma_start(bf_row[:], bf.rearrange("(a e) -> a e", a=1).broadcast_to((P, D))).then_inc(consts_loaded, 16)
            sp.dma_start(adj_in[:, 0], adj_v[0]).then_inc(adj_loaded[0], 16)
            for name in w_late:
                sp.dma_start(staged[name], w_source[name].rearrange("(c p) n -> p c n", p=P)).then_inc(w_loaded[name], 16)

            def body(i, par):
                j = i - 1
                if real(i + 1):
                    load_x(i + 1, 1 - par)
                if real(i):
                    sp.wait_ge(values0_made, (i + 1) * TILES)
                    sp.sem_inc(sp_passed, 1)
                    if real(i - 1):
                        sp.wait_ge(attn0_full, 2 * i)
                        sp.sem_inc(sp_passed, 1)
                    else:
                        sp.wait_ge(ones_made, 4)
                    for g in range(2):
                        for o in range(2):
                            sp.dma_start(V0[64 * o:64 * o + 64, g, :, o, 0:E0].rearrange("p t e k -> p t (e k)"),
                                         x1[64 * g:64 * g + 64, :, o * D // 2:(o + 1) * D // 2]).then_inc(values0_spread, 16)
                if real(i):
                    sp.wait_ge(srcdst_copied, i + 1)
                    sp.sem_inc(sp_passed, 1)
                    sp.dma_start(d_scratch[i].rearrange("g h m -> h g m"),
                                 sdT[0:HEADS0, :].rearrange("h (g m) -> h g m", m=N)).then_inc(dst_stored, 16)
                    sp.wait_ge(dst_stored, 16 * (i + 1))
                    sp.sem_inc(sp_passed, 1)
                    if real(i - 1):
                        sp.wait_ge(probs0_turned, 6 * i)
                        sp.sem_inc(sp_passed, 1)
                    else:
                        sp.wait_ge(w_low, 3 * C)
                    for g in range(2):
                        src = d_scratch[i].rearrange("(t g) h m -> g t (h m)", g=2)[g:g + 1]
                        sp.dma_start(z[64 * g:64 * g + 64], src.broadcast_to((64, TILES, HEADS0 * N))).then_inc(dst_spread, 16)
                if real(j):
                    sp.wait_ge(values1_made, (j + 1) * TILES)
                    sp.sem_inc(sp_passed, 1)
                    if real(j - 1):
                        sp.wait_ge(attn1_full, 2 * j)
                        sp.sem_inc(sp_passed, 1)
                    for g in range(2):
                        for o in range(2):
                            sp.dma_start(V1[64 * o:64 * o + 64, g, :, o, 0:E1].rearrange("p t e k -> p t (e k)"),
                                         x1[64 * g:64 * g + 64, :, o * D // 2:(o + 1) * D // 2]).then_inc(values1_spread, 16)
                if real(j):
                    sp.wait_ge(out_made, (j + 1) * TILES)
                    sp.sem_inc(sp_passed, 1)
                    sp.dma_start(out_v[j], x2[:]).then_inc(out_stored, 16)

            iterations(sp, body)
            sp.wait_ge(out_stored, 16 * groups)

        @block.gpsimd
        def _(pool):
            pool.memset(ident[:], 0.0).then_inc(zeros_made, 1)
            pool.memset(ident_b[:], 0.0).then_inc(zeros_made, 1)
            pool.memset(wsd[:], 0.0).then_inc(consts_made, 1)
            pool.memset(hb_rows[:].bitcast(F32), 0.0).then_inc(consts_made, 1)
            pool.memset(masked0[:], MASKED0).then_inc(consts_made, 1)
            pool.memset(minus1[:], -1.0).then_inc(consts_made, 1)
            pool.memset(half[:], 0.5).then_inc(consts_made, 1)
            pool.memset(minus_half[:], -0.5).then_inc(consts_made, 1)
            pool.wait_ge(zeros_made, 2)
            for m in (ident, ident_b):
                pool.affine_select(out=m[:], in_=m[:], compare_op=ALU.not_equal, fill=1.0, base=0,
                                   pattern=[[-1, P]], channel_multiplier=1).then_inc(consts_made, 1)
            pool.wait_ge(consts_made, 8)

            def inv_std(layer, g):
                pool.wait_ge((moments0, moments1)[layer], TILES * (g + 1))
                pool.sem_inc(pool_passed, 1)
                pool.tensor_scalar(ve[:, layer], mv[:, layer, :, 1], EPS, None, ALU.add).then_inc((var0_eps, var1_eps)[layer], 1)
                pool.wait_ge((var0_eps, var1_eps)[layer], g + 1)
                if real(g - 1):
                    pool.wait_ge((xn0_made, xn1_made)[layer], TILES * g)
                pool.tensor_tensor(rstd[:, layer], ve[:, layer], minus_half[:], ALU.pow).then_inc((inv_std0, inv_std1)[layer], 1)

            inv_std(0, 0)
            pool.memset(V0[:], 0.0).then_inc(zeros_made, 1)
            pool.memset(V1[:], 0.0).then_inc(zeros_made, 1)
            pool.memset(K_blocks[:], 0.0).then_inc(k_zeros_made, 1)
            pool.wait_ge(k_zeros_made, 1)
            pool.wait_ge(zeros_made, 4)
            for o in range(2):
                rows = slice(64 * o, 64 * o + 64)
                pool.memset(V0[rows, :, :, o, E0], 1.0).then_inc(ones_made, 1)
                pool.memset(V1[rows, :, :, o, E1], 1.0).then_inc(ones_made, 1)
            pool.wait_ge(ones_made, 4)

            def body(i, par):
                if not real(i):
                    return
                if real(i + 1):
                    inv_std(0, i + 1)
                pool.wait_ge(dst_spread, 32 * (i + 1))
                pool.wait_ge(src_copied, i + 1)
                for t in range(TILES):
                    zt = z[:, t].rearrange("p (h m) -> p h m", m=N)
                    pool.tensor_tensor(zt, zt, s_tok[:, t, HEADS0:].unsqueeze(2).broadcast_to((P, HEADS0, N)),
                                       ALU.add).then_inc(scores0_summed, 1)
                if real(i - 1):
                    pool.wait_ge(out_stored, 16 * i)
                for t in range(TILES):
                    pool.wait_ge(gated, TILES * i + t + 1)
                    pool.tensor_tensor(x2[:, t], x_in[:, par, t], ee[:, t], ALU.subtract).then_inc(x2_made, 1)
                inv_std(1, i)
                pool.wait_ge(xn1_made, TILES * (i + 1))
                for t in range(TILES):
                    pool.tensor_tensor(x2[:, t], x2[:, t], bf_row[:], ALU.add).then_inc(x2_biased, 1)

            iterations(pool, body)

        @block.scalar
        def _(act):
            def h0_parts(g):
                if real(g - 1):
                    act.wait_ge(gate_full, TILES * g)
                for c in range(C):
                    act.wait_ge(xn0_turned, C * g + c + 1)
                    act.activation(hT0h[:, c], ps[:, job("h0_low", c) % BANKS], ACT.Relu).then_inc(h0_high, 1)

            act.wait_ge(hw_turned, 3)
            for c in range(C):
                act.activation(wh["Hw"][:, c, :], ps[:, 1 + c, 0:D], ACT.Copy).then_inc(w_high, 1)
            act.wait_ge(w_loaded["W0"], 16 * C)
            for c in range(C):
                act.activation(wh["W0"][:, c, :], staged["W0"][:, c], ACT.Copy).then_inc(w0_high, 1)
            h0_parts(0)
            act.wait_ge(consts_loaded, 16 * 9)
            act.wait_ge(consts_made, 8)
            for r in (0, 32):
                act.activation(hb_rows[r:r + 1, :], x2[r:r + 1, 0, :], ACT.Copy).then_inc(rows_made, 1)
            act.activation(ones_rows[:], ident[0:33, :], ACT.Identity, scale=0.0, bias=1.0).then_inc(rows_made, 1)
            for name in w_late:
                act.wait_ge(w_loaded[name], 16)
                for c in range(C):
                    act.activation(wh[name][:, c, :], staged[name][:, c], ACT.Copy).then_inc(w_high, 1)

            def body(i, par):
                j = i - 1
                if real(i):
                    for t in range(TILES):
                        act.wait_ge(values0_made, TILES * i + t + 1)
                        if real(i - 1):
                            act.wait_ge(x2_made, TILES * (i - 1) + t + 1)
                        act.activation(ee[:, t], ps[:, job("th_made", t) % BANKS, 0:D], ACT.Tanh).then_inc(th_made, 1)
                        act.wait_ge(gate_full, TILES * i + t + 1)
                        if real(i - 1):
                            act.wait_ge(gated, TILES * (i - 1) + t + 1)
                        act.activation(gate[:, t], ps[:, job("gate_tanh", t) % BANKS, 0:D], ACT.Tanh, scale=0.5).then_inc(gate_tanh, 1)
                if real(j):
                    if real(j - 1):
                        act.wait_ge(final_full, TILES * j)
                    for c in range(C):
                        act.wait_ge(xn1_turned, C * j + c + 1)
                        act.activation(hT1h[:, c], ps[:, job("h1_low", c) % BANKS], ACT.Relu).then_inc(h1_high, 1)
                if real(i):
                    if real(i - 1):
                        act.wait_ge(attn0_full, 2 * i)
                    else:
                        act.wait_ge(w_low, C)
                    for c in range(C):
                        act.wait_ge(th_turned, C * i + c + 1)
                        act.activation(thT[:, c], ps[:, job("thT_copied", c) % BANKS], ACT.Copy).then_inc(thT_copied, 1)

                def copy_q(c):
                    act.wait_ge(q_full, C * j + c + 1)
                    act.activation(QT[:, c], ps[:, job("q_copied", c) % BANKS], ACT.Identity,
                                   bias=bq_col[:, c:c + 1]).then_inc(q_copied, 1)

                def copy_k(c):
                    act.wait_ge(k_full, C * j + c + 1)
                    for o in range(2):
                        rows = slice(64 * o, 64 * o + 64)
                        act.activation(K_blocks[rows, c, :, o], ps[rows, job("k_copied", c) % BANKS].rearrange("p (g m) -> p g m", m=N),
                                       ACT.Identity, bias=bk_col[rows, c:c + 1]).then_inc(k_copied, 1)

                if real(j):
                    act.wait_ge(attn0_full, 2 * (j + 1))
                    copy_q(0)
                if real(i):
                    act.wait_ge(srcdst_full, i + 1)
                    if real(i - 1):
                        act.wait_ge(dst_stored, 16 * i)
                    act.activation(sdT[:], ps[0:2 * HEADS0, job("src_copied", 0) % BANKS], ACT.Copy).then_inc(srcdst_copied, 1)
                if real(j):
                    copy_q(1)
                    copy_q(2)
                if real(i + 1):
                    h0_parts(i + 1)
                if real(j):
                    if not real(j - 1):
                        act.wait_ge(k_zeros_made, 1)
                    for c in range(C):
                        copy_k(c)
                if real(i):
                    for t in range(TILES):
                        act.wait_ge(gate_tanh, TILES * i + t + 1)
                        act.activation(gate[:, t], gate[:, t], ACT.Identity, scale=0.5, bias=half[:]).then_inc(gate_made, 1)

                def exp0(t):
                    if real(i):
                        act.wait_ge(scores0_shifted, TILES * i + t + 1)
                        act.activation(z[:, t], z[:, t], ACT.Exp).then_inc(probs0_made, 1)

                def exp1(t):
                    if real(j):
                        act.wait_ge(scores1_shifted, TILES * j + t + 1)
                        act.activation(p1[:, t], p1[:, t], ACT.Exp, scale=float(E1) ** -0.5).then_inc(probs1_made, 1)

                exp0(0)
                exp0(1)
                exp1(0)
                exp1(1)
                exp1(2)
                exp1(3)
                if real(j):
                    if real(i):
                        act.wait_ge(srcdst_full, i + 1)
                    for c in range(3):
                        act.wait_ge(probs1_turned, 3 * j + c + 1)
                        act.activation(thT[:, c], ps[:, job("probs1T_copied", c) % BANKS], ACT.Copy).then_inc(probs1T_copied, 1)
                exp0(2)
                exp0(3)
                if real(i):
                    if real(i - 1):
                        act.wait_ge(scores1_full, 2 * i)
                        act.wait_ge(attn1_full, 2 * i)
                    for q in range(6):
                        act.wait_ge(probs0_turned, 6 * i + q + 1)
                        act.activation((QT[:, q] if q < 3 else thT[:, q - 3]), ps[:, job("probs0T_copied", q) % BANKS], ACT.Copy).then_inc(probs0T_copied, 1)
                if real(j):
                    act.wait_ge(values1_full, TILES * (j + 1))
                    for c in range(C):
                        act.wait_ge(attn1_turned, C * j + c + 1)
                        act.activation(hT1h[:, c], ps[:, job("attn1_low", c) % BANKS], ACT.Copy).then_inc(attn1_high, 1)
                if real(i):
                    for t in range(TILES):
                        act.wait_ge(attn0_made, TILES * i + t + 1)
                        act.activation(ee[:, t], x1[:, t], ACT.Exp, bias=minus1[:]).then_inc(elu_exp, 1)

            iterations(act, body)

        @block.tensor
        def _(pe):
            def turn(dst, src, rows=P):
                return pe.transpose(dst, src, ident[0:rows, 0:rows])

            def take(i, at):
                reader = last_reader(i, at)
                if reader is not None:
                    pe.wait_ge(*reader)
                return ps[:, at % BANKS]

            def product(dst, left_h, left_l, right_h, right_l, more=False, chunk_ready=None):
                for c in range(C):
                    if chunk_ready is not None:
                        pe.wait_ge(*chunk_ready(c))
                    pe.matmul(dst, left_h(c), right_h(c), start=(c == 0), stop=False)
                    pe.matmul(dst, left_h(c), right_l(c), start=False, stop=False)
                    mm = pe.matmul(dst, left_l(c), right_h(c), start=False, stop=(c == C - 1 and not more))
                return mm

            pe.wait_ge(consts_made, 8)
            pe.wait_ge(hw_loaded, 16)
            for c in range(C):
                for f in range(C):
                    mm = turn(ps[:, 1 + c, f * P:(f + 1) * P], staged["Hw"][:, f, c * P:(c + 1) * P])
                mm.then_inc(hw_turned, 1)

            def turn_tokens(name, done, src, i, g):
                for c in range(C):
                    take(i, job(name, c))
                    for t in range(TILES):
                        mm = turn(ps[:, job(name, c) % BANKS, t * P:(t + 1) * P], src(t, c))
                    mm.then_inc(done, 1)

            def turn_h0(it, g, par):
                pe.wait_ge(xn0_made, TILES * (g + 1))
                turn_tokens("h0_low", xn0_turned, lambda t, c: xn0[:, par, t, c * P:(c + 1) * P], it, g)

            turn_h0(NEXT, 0, 0)
            pe.wait_ge(small_ready, 5)
            pe.wait_ge(rows_made, 3)
            pe.wait_ge(w0_low, C)

            def body(i, par):
                j = i - 1
                if real(i):
                    pe.wait_ge(h0_low, C * (i + 1))
                    for t in range(TILES):
                        toks = slice(t * P, (t + 1) * P)
                        take(i, job("th_made", t))
                        product(ps[:, job("th_made", t) % BANKS, 0:D], lambda c: hT0h[:, c, toks], lambda c: hT0l[:, c, toks],
                                lambda c: wh["W0"][:, c], lambda c: wl["W0"][:, c]).then_inc(values0_full, 1)
                        take(i, job("gate_tanh", t))
                        dst = ps[:, job("gate_tanh", t) % BANKS, 0:D]
                        product(dst, lambda c: hT0h[:, c, toks], lambda c: hT0l[:, c, toks],
                                lambda c: wh["Hw"][:, c], lambda c: wl["Hw"][:, c], more=True)
                        pe.matmul(dst, ones_rows[:], hb_rows[:], start=False, stop=True).then_inc(gate_full, 1)
                if real(j):
                    pe.wait_ge(xn1_made, TILES * (j + 1))
                    turn_tokens("h1_low", xn1_turned, lambda t, c: p1[:, t, c * P:(c + 1) * P], i, j)
                if real(i):
                    pe.wait_ge(th_made, TILES * (i + 1))
                    turn_tokens("thT_copied", th_turned, lambda t, c: ee[:, t, c * P:(c + 1) * P], i, i)

                def project(o, full, name, w):
                    take(i, job(name, o))
                    cols = slice(o * P, (o + 1) * P)
                    product(ps[:, job(name, o) % BANKS], lambda c: wh[w][:, c, cols], lambda c: wl[w][:, c, cols],
                            lambda c: hT1h[:, c], lambda c: hT1l[:, c],
                            chunk_ready=lambda c: (h1_low, C * j + c + 1)).then_inc(full, 1)

                if real(j):
                    if not real(j - 1):
                        pe.wait_ge(w_low, C * 4)
                    project(0, q_full, "q_copied", "Wq")
                if real(i):
                    pe.wait_ge(thT_copied, C * (i + 1))
                    take(i, job("src_copied", 0))
                    for c in range(C):
                        mm = pe.matmul(ps[0:2 * HEADS0, job("src_copied", 0) % BANKS], wsd[:, c], thT[:, c],
                                       start=(c == 0), stop=(c == C - 1))
                    mm.then_inc(srcdst_full, 1)
                if real(j):
                    project(1, q_full, "q_copied", "Wq")
                    project(2, q_full, "q_copied", "Wq")
                if real(i):
                    pe.wait_ge(srcdst_copied, i + 1)
                    pe.sem_inc(pe_passed, 1)
                    for t in range(TILES):
                        mm = turn(ps[:, job("src_copied", 0) % BANKS, t * 2 * HEADS0:(t + 1) * 2 * HEADS0],
                                  sdT[:, t * P:(t + 1) * P], 2 * HEADS0)
                    mm.then_inc(srcdst_turned, 1)
                def values1(t):
                    toks = slice(t * P, (t + 1) * P)
                    take(i, job("values1_made", t))
                    product(ps[:, job("values1_made", t) % BANKS, 0:D], lambda c: hT1h[:, c, toks], lambda c: hT1l[:, c, toks],
                            lambda c: wh["Wv"][:, c], lambda c: wl["Wv"][:, c]).then_inc(values1_full, 1)

                if real(j):
                    values1(0)
                    values1(1)
                    values1(2)
                    values1(3)
                if real(i + 1):
                    turn_h0(i, i + 1, 1 - par)
                if real(j):
                    project(0, k_full, "k_copied", "Wk")
                    project(1, k_full, "k_copied", "Wk")
                    project(2, k_full, "k_copied", "Wk")
                def scores(pair):
                    for t in (2 * pair, 2 * pair + 1):
                        take(i, job("scores1_shifted", t))
                        bank = ps[:, job("scores1_shifted", t) % BANKS, 0:D]
                        pe.matmul(bank.rearrange("p (h m) -> p h m", m=N), ident_b[:],
                                  mask1[:, t].unsqueeze(1).broadcast_to((P, HEADS1, N)),
                                  start=True, stop=False, skip_group_check=True)
                        for k in range(PAIRS1):
                            for g in range(2):
                                at = t * P + g * N
                                mm = pe.matmul(bank[g * N:(g + 1) * N, k * P:(k + 1) * P], QT[:, k, at:at + N],
                                               K_blocks[:, k, 2 * t + g].rearrange("p o m -> p (o m)"),
                                               start=False, stop=True, skip_group_check=True)
                    mm.then_inc(scores1_full, 1)

                if real(j):
                    pe.wait_ge(q_copied, C * (j + 1))
                    pe.wait_ge(k_copied, 2 * C * (j + 1))
                    pe.wait_ge(mask1_made, j + 1)
                    scores(0)
                    scores(1)

                def turn_probs(name, ready, done, src, pairs, g, jobs):
                    for q in range(jobs):
                        take(i, job(name, q))
                        for k in range(4):
                            t, pair = divmod(4 * q + k, pairs)
                            if k == 0 or pair == 0:
                                pe.wait_ge(ready, TILES * g + t + 1)
                            mm = turn(ps[:, job(name, q) % BANKS, k * P:(k + 1) * P], src[:, t, pair * P:(pair + 1) * P])
                        mm.then_inc(done, 1)

                def attend(pair, name, done, ready, spread, probsT, V, heads, width, g_, ready_n):
                    pairs = heads // 2
                    last = ((2 * pair + 2) * pairs - 1) // 4
                    pe.wait_ge(spread, 64 * (g_ + 1))
                    pe.sem_inc(pe_passed, 1)
                    pe.wait_ge(ready, ready_n * g_ + last + 1)
                    pe.sem_inc(pe_passed, 1)
                    for t in (2 * pair, 2 * pair + 1):
                        take(i, job(name, t))
                        pe.sem_inc(pe_passed, 1)
                        bank = ps[:, job(name, t) % BANKS, 0:heads * (width + 1)].rearrange("p (k o e) -> p k o e", o=2, e=width + 1)
                        for pair_of_heads in range(pairs):
                            q, k = divmod(t * pairs + pair_of_heads, 4)
                            for g in range(2):
                                mm = pe.matmul(bank[g * N:(g + 1) * N, pair_of_heads],
                                               probsT(q)[:, k * P + g * N:k * P + (g + 1) * N],
                                               V[:, g, t, :, :, pair_of_heads], start=True, stop=True, skip_group_check=True)
                    mm.then_inc(done, 1)

                if not real(j):
                    pe.wait_ge(ones_made, 4)

                def attend1(pair):
                    attend(pair, "attn1_made", attn1_full, probs1T_copied, values1_spread, lambda q: thT[:, q], V1, HEADS1, E1, j, 3)

                def attend0(pair):
                    attend(pair, "attn0_made", attn0_full, probs0T_copied, values0_spread, lambda q: QT[:, q] if q < 3 else thT[:, q - 3], V0, HEADS0, E0, i, 6)

                if real(j):
                    turn_probs("probs1T_copied", probs1_made, probs1_turned, p1, PAIRS1, j, 3)
                    attend1(0)
                    attend1(1)
                if real(i):
                    turn_probs("probs0T_copied", probs0_made, probs0_turned, z, PAIRS0, i, 6)
                    attend0(0)
                if real(j):
                    pe.wait_ge(attn1_made, TILES * (j + 1))
                    turn_tokens("attn1_low", attn1_turned, lambda t, c: p1[:, t, c * P:(c + 1) * P], i, j)
                    for t in range(TILES):
                        toks = slice(t * P, (t + 1) * P)
                        take(i, job("out_made", t))
                        product(ps[:, job("out_made", t) % BANKS, 0:D], lambda c: hT1h[:, c, toks], lambda c: hT1l[:, c, toks],
                                lambda c: wh["Wf"][:, c], lambda c: wl["Wf"][:, c],
                                chunk_ready=lambda c: (attn1_low, C * j + c + 1)).then_inc(final_full, 1)
                if real(i):
                    attend0(1)

            iterations(pe, body)

        @block.vector
        def _(dve):
            def row_stats(layer, src, t, g):
                dve.bn_stats(stats[:, layer, t], src).then_inc((stats0, stats1)[layer], 1)

            def row_sums(layer, g):
                for t in range(TILES):
                    dve.wait_ge((stats0, stats1)[layer], TILES * g + t + 1)
                    dve.sem_inc(dve_passed, 1)
                    dve.bn_aggr(mv[:, layer, t], stats[:, layer, t]).then_inc((moments0, moments1)[layer], 1)

            def normalise(layer, src, dst, done, g):
                dve.wait_ge((inv_std0, inv_std1)[layer], g + 1)
                for t in range(TILES):
                    dve.tensor_scalar(dst(t), src(t), mv[:, layer, t, 0:1], rstd[:, layer, t:t + 1],
                                      ALU.subtract, ALU.mult).then_inc(done, 1)

            def norm0(g, par):
                dve.wait_ge(x_loaded[par], 8 * (g - par) + 16)
                for t in range(TILES):
                    row_stats(0, x_in[:, par, t], t, g)
                row_sums(0, g)

            def norm0_end(g, par):
                normalise(0, lambda t: x_in[:, par, t], lambda t: xn0[:, par, t], xn0_made, g)

            def h0_lows(g):
                for c in range(C):
                    dve.wait_ge(h0_high, C * g + c + 1)
                    dve.scalar_tensor_tensor(hT0l[:, c], ps[:, job("h0_low", c) % BANKS], 0.0, hT0h[:, c].bitcast(F32),
                                             ALU.max, ALU.subtract).then_inc(h0_low, 1)

            norm0(0, 0)
            norm0_end(0, 0)
            for c in range(C):
                dve.wait_ge(w_high, c + 1)
                dve.tensor_tensor(wl["Hw"][:, c, :], ps[:, 1 + c, 0:D], wh["Hw"][:, c, :].bitcast(F32), ALU.subtract)\
                    .then_inc(small_ready, 1)
            for c in range(C):
                dve.wait_ge(w0_high, c + 1)
                dve.tensor_tensor(wl["W0"][:, c, :], staged["W0"][:, c], wh["W0"][:, c, :].bitcast(F32),
                                  ALU.subtract).then_inc(w0_low, 1)
            h0_lows(0)
            dve.wait_ge(consts_loaded, 16 * 9)
            dve.wait_ge(consts_made, 8)
            dve.wait_ge(rows_made, 2)
            dve.tensor_tensor(hb_rows[32:33, :], x2[32:33, 0, :], hb_rows[32:33, :].bitcast(F32), ALU.subtract)\
                .then_inc(small_ready, 1)
            for k, col in ((0, wcol), (HEADS0, wcol2)):
                for q in range(4):
                    rows = slice(32 * q, 32 * q + 32)
                    for c in range(C):
                        at = k + 4 * c + q
                        dve.tensor_copy(wsd[rows, c, at:at + 1], col[rows, c:c + 1])
            dve.tensor_scalar(b0_plus1[:], b0_plus1[:], 1.0, None, ALU.add).then_inc(small_ready, 1)
            for n, name in enumerate(w_late):
                for c in range(C):
                    dve.wait_ge(w_high, C * (n + 1) + c + 1)
                    dve.tensor_tensor(wl[name][:, c, :], staged[name][:, c], wh[name][:, c, :].bitcast(F32),
                                      ALU.subtract).then_inc(w_low, 1)
            dve.wait_ge(small_ready, 5)

            def body(i, par):
                j = i - 1
                if real(i):
                    for t in range(TILES):
                        dve.wait_ge(values0_full, TILES * i + t + 1)
                        dve.tensor_tensor(x1[:, t].rearrange("p (o e k) -> p k o e", o=2, e=E0),
                                          ps[:, job("th_made", t) % BANKS, 0:D].rearrange("p (k o e) -> p k o e", o=2, e=E0),
                                          b0_plus1[:].unsqueeze(1).unsqueeze(1).broadcast_to((P, PAIRS0, 2, E0)), ALU.add)\
                            .then_inc(values0_made, 1)
                    dve.wait_ge(adj_loaded[par], 8 * (i - par) + 16)
                    if real(i - 1):
                        dve.wait_ge(masked, TILES * i)
                    dve.tensor_scalar(not_adj[:], adj_in[:, par], 0.0, None, ALU.is_equal).then_inc(not_adj_made, 1)
                if real(j):
                    for c in range(C):
                        dve.wait_ge(h1_high, C * j + c + 1)
                        dve.scalar_tensor_tensor(hT1l[:, c], ps[:, job("h1_low", c) % BANKS], 0.0, hT1h[:, c].bitcast(F32),
                                                 ALU.max, ALU.subtract).then_inc(h1_low, 1)
                if real(i + 1):
                    norm0(i + 1, 1 - par)
                    norm0_end(i + 1, 1 - par)
                if real(i):
                    dve.wait_ge(srcdst_turned, i + 1)
                    if real(i - 1):
                        dve.wait_ge(scores0_summed, TILES * i)
                    dve.tensor_copy(s_tok[:].rearrange("p t h -> p (t h)"),
                                    ps[:, job("src_copied", 0) % BANKS, 0:TILES * 2 * HEADS0]).then_inc(src_copied, 1)

                def values1(t):
                    if real(j):
                        dve.wait_ge(values1_full, TILES * j + t + 1)
                        dve.tensor_tensor(x1[:, t].rearrange("p (o e k) -> p k o e", o=2, e=E1),
                                          ps[:, job("values1_made", t) % BANKS, 0:D].rearrange("p (k o e) -> p k o e", o=2, e=E1),
                                          bv_row[:].rearrange("p (k o e) -> p k o e", o=2, e=E1), ALU.add).then_inc(values1_made, 1)

                def shift1(pair):
                    dve.wait_ge(scores1_full, 2 * j + pair + 1)
                    for t in (2 * pair, 2 * pair + 1):
                        bank = ps[:, job("scores1_shifted", t) % BANKS, 0:D].rearrange("p (h m) -> p h m", m=N)
                        dve.tensor_reduce(mx1[:, t], bank, AX_X, ALU.max).then_inc(max1_made, 1)
                        dve.wait_ge(max1_made, TILES * j + t + 1)
                        dve.tensor_tensor(p1[:, t].rearrange("p (h m) -> p h m", m=N), bank,
                                          mx1[:, t].unsqueeze(2).broadcast_to((P, HEADS1, N)), ALU.subtract)\
                            .then_inc(scores1_shifted, 1)

                def softmax0(t):
                    n = TILES * i + t + 1
                    zt = z[:, t].rearrange("p (h m) -> p h m", m=N)
                    dve.wait_ge(scores0_summed, n)
                    dve.scalar_tensor_tensor(z[:, t], z[:, t], SLOPE, z[:, t], ALU.mult, ALU.max).then_inc(leaky_made, 1)
                    dve.wait_ge(leaky_made, n)
                    dve.sem_inc(dve_passed, 1)
                    dve.wait_ge(not_adj_made, i + 1)
                    dve.sem_inc(dve_passed, 1)
                    dve.copy_predicated(zt, not_adj[:, t].unsqueeze(1).broadcast_to((P, HEADS0, N)),
                                        masked0[:].unsqueeze(2).broadcast_to((P, HEADS0, N))).then_inc(masked, 1)
                    dve.wait_ge(masked, n)
                    dve.tensor_reduce(mx0[:, t], zt, AX_X, ALU.max).then_inc(max0_made, 1)
                    dve.wait_ge(max0_made, n)
                    dve.tensor_tensor(zt, zt, mx0[:, t].unsqueeze(2).broadcast_to((P, HEADS0, N)), ALU.subtract)\
                        .then_inc(scores0_shifted, 1)

                def divide(t, name, full, dst, sums, inverted, done, heads, width, g):
                    v = ps[:, job(name, t) % BANKS, 0:heads * (width + 1)].rearrange("p (h e) -> p h e", e=width + 1)
                    dve.wait_ge(full, 2 * g + t // 2 + 1)
                    dve.reciprocal(sums[:, t], v[:, :, width]).then_inc(inverted, 1)
                    dve.wait_ge(inverted, 4 * g + t + 1)
                    dve.tensor_tensor(dst[:, t].rearrange("p (h e) -> p h e", e=width), v[:, :, 0:width],
                                      sums[:, t].unsqueeze(2).broadcast_to((P, heads, width)), ALU.mult).then_inc(done, 1)

                def close(t):
                    n = TILES * i + t + 1
                    dve.wait_ge(elu_exp, n)
                    dve.scalar_tensor_tensor(ee[:, t], ee[:, t], 1.0, x1[:, t], ALU.min, ALU.max).then_inc(elu_made, 1)
                    dve.scalar_tensor_tensor(x_in[:, par, t], xn0[:, par, t], 0.0, x_in[:, par, t], ALU.max, ALU.add)\
                        .then_inc(x_plus_h, 1)
                    dve.wait_ge(elu_made, n)
                    dve.scalar_tensor_tensor(x1[:, t], xn0[:, par, t], 0.0, ee[:, t], ALU.max, ALU.subtract)\
                        .then_inc(h_less_elu, 1)
                    dve.wait_ge(h_less_elu, n)
                    dve.wait_ge(x_plus_h, n)
                    dve.wait_ge(gate_made, n)
                    dve.scalar_tensor_tensor(ee[:, t], x1[:, t], 1.0, gate[:, t], ALU.add, ALU.mult).then_inc(gated, 1)

                def divide0(pair):
                    for t in (2 * pair, 2 * pair + 1):
                        divide(t, "attn0_made", attn0_full, x1, rs0, inv0_made, attn0_made, HEADS0, E0, i)

                def add_out(t):
                    if real(j):
                        dve.wait_ge(final_full, TILES * j + t + 1)
                        dve.tensor_tensor(x2[:, t],
                                          ps[:, job("out_made", t) % BANKS, 0:D], x2[:, t], ALU.add).then_inc(out_made, 1)

                def divide1(pair):
                    for t in (2 * pair, 2 * pair + 1):
                        divide(t, "attn1_made", attn1_full, p1, rs1, inv1_made, attn1_made, HEADS1, E1, j)

                if real(j):
                    if real(i):
                        dve.wait_ge(values0_spread, 64 * (i + 1))
                    values1(0)
                    values1(1)
                    values1(2)
                    values1(3)
                if real(i + 1):
                    h0_lows(i + 1)
                if real(i):
                    softmax0(0)
                    softmax0(1)
                if real(j):
                    shift1(0)
                    shift1(1)
                if real(i):
                    softmax0(2)
                    softmax0(3)
                    if real(j):
                        dve.wait_ge(scores1_full, 2 * (j + 1))
                    dve.tensor_scalar(mask1[:], adj_in[:, par], -1.0, MASKED1 * float(E1) ** 0.5, ALU.add, ALU.mult)\
                        .then_inc(mask1_made, 1)
                if real(j):
                    dve.wait_ge(probs1_turned, 3 * (j + 1))
                    divide1(0)
                    divide1(1)
                if real(j) and real(i):
                    dve.wait_ge(values1_spread, 64 * (j + 1))
                if real(i):
                    divide0(0)
                if real(j):
                    for c in range(C):
                        dve.wait_ge(attn1_high, C * j + c + 1)
                        dve.tensor_tensor(hT1l[:, c], ps[:, job("attn1_low", c) % BANKS], hT1h[:, c].bitcast(F32), ALU.subtract)\
                            .then_inc(attn1_low, 1)
                    dve.wait_ge(x2_biased, TILES * (j + 1))
                if real(i):
                    close(0)
                add_out(0)
                add_out(1)
                if real(i):
                    close(1)
                add_out(2)
                add_out(3)
                if real(i):
                    divide0(1)
                    close(2)
                    close(3)
                    for t in range(TILES):
                        dve.wait_ge(x2_made, TILES * i + t + 1)
                        row_stats(1, x2[:, t], t, i)
                    row_sums(1, i)
                    if real(j):
                        dve.wait_ge(attn1_turned, C * (j + 1))
                    normalise(1, lambda t: x2[:, t], lambda t: p1[:, t], xn1_made, i)

            iterations(dve, body)


_INS = ['x', 'adj', 'L0_gnn_W', 'L0_gnn_b', 'L0_gnn_w_src', 'L0_gnn_w_dst', 'L0_gnn_H_w', 'L0_gnn_H_b', 'L1_gnn_Wq',
        'L1_gnn_bq', 'L1_gnn_Wk', 'L1_gnn_bk', 'L1_gnn_Wv', 'L1_gnn_bv', 'L1_gnn_Wf', 'L1_gnn_bf']


def kernel(**inputs):
    import concourse.bacc as _bacc
    from concourse.bass_utils import run_bass_kernel_spmd as _run

    nc = _bacc.Bacc("TRN2", target_bir_lowering=False, num_devices=1)
    arrays, args = {}, []
    for name in _INS:
        a = np.ascontiguousarray(inputs[name])
        arrays[f"in_{name}_dram"] = a
        args.append(nc.dram_tensor(f"in_{name}_dram", a.shape, mybir.dt.from_np(a.dtype), kind="ExternalInput").ap())
    shape = np.shape(inputs['x'])
    graphs = 2 * TILES
    out = nc.dram_tensor("out_0_dram", shape, F32, kind="ExternalOutput").ap()
    scratch = nc.dram_tensor("d_scratch", (shape[0] // graphs, graphs, HEADS0, N), F32, kind="Internal").ap()
    two_layer_gnn(nc, *args, out, scratch)
    r = _run(nc, [arrays], core_ids=[0])
    return r.results[0]["out_0_dram"]
```
